# Optimizing a Trainium2 kernel written in Bass

```python
import numpy as np
import jax
import jax.numpy as jnp

def _softmax(x, axis=-1):
    return jax.nn.softmax(x, axis=axis)

def _gelu(x):
    return jax.nn.gelu(x, approximate=True)

def _silu(x):
    return jax.nn.silu(x)

def _sigmoid(x):
    return jax.nn.sigmoid(x)

def _layernorm(x, axis=-1, eps=1e-05):
    m = jnp.mean(x, axis=axis, keepdims=True)
    v = jnp.var(x, axis=axis, keepdims=True)
    return (x - m) / jnp.sqrt(v + eps)

def _scatter_add(tgt, idx, src, axis=0):
    return tgt.at[idx].add(src)

def _segment_sum(src, seg, n):
    return jax.ops.segment_sum(src, seg, n)
kernel_name = 'mk_gnn_resnorm_d2_gnn_r8_f88b37'

def setup_inputs(seed: int=0):
    np.random.seed(seed)
    _w = jnp.asarray

    def _rec_inputs():
        import jax
        import jax.numpy as jnp
        _gk = jax.random.key(seed)
        x = -0.0002117 + 1 * jax.random.normal(jax.random.fold_in(_gk, 1), (6250, 256), jnp.float32)
        src = jax.random.randint(jax.random.fold_in(_gk, 2), (100000,), 0, 6250, jnp.int32)
        dst = jax.random.randint(jax.random.fold_in(_gk, 3), (100000,), 0, 6250, jnp.int32)
        _o = jnp.argsort(dst, stable=True)
        src = src[_o]
        dst = dst[_o]
        edge_type_500 = jax.random.randint(jax.random.fold_in(_gk, 12), (100000,), 0, 500, jnp.int32)
        return (x, src, dst, edge_type_500)
    x, src, dst, edge_type_500 = _rec_inputs()

    def _L0_gnn_setup():
        import jax, jax.numpy as jnp
        import numpy as np
        G = (1.0, 1.0)

        def to_hypercomplex(x, n_blades):
            return x.reshape(*x.shape[:-1], n_blades, -1).swapaxes(-2, -1)

        def clifford_kernel_2d(w, g):
            g0, g1 = g
            k0 = jnp.concatenate([w[0], g0 * w[1], g1 * w[2], -g0 * g1 * w[3]], axis=1)
            k1 = jnp.concatenate([w[1], w[0], -g1 * w[3], g1 * w[2]], axis=1)
            k2 = jnp.concatenate([w[2], g0 * w[3], w[0], -g0 * w[1]], axis=1)
            k3 = jnp.concatenate([w[3], w[2], w[1], w[0]], axis=1)
            return jnp.concatenate([k0, k1, k2, k3], axis=0)

        def clifford_linear(x, w, b, g=G):
            N = x.shape[0]
            k = clifford_kernel_2d(w, g)
            xf = x.swapaxes(-2, -1).reshape(N, -1)
            out = xf @ k.T + b.reshape(-1)
            C_out = w.shape[1]
            return out.reshape(N, 4, C_out).swapaxes(-2, -1)
        key = jax.random.key(seed)
        ks = jax.random.split(key, 10)
        N, E, R, emb_dim = (12500, 75000, 500, 256)
        C = emb_dim // 4
        s = 0.05
        return {'h': jax.random.normal(ks[0], (N, emb_dim), jnp.float32), 'edge_index': jax.random.randint(ks[1], (2, E), 0, N, jnp.int64), 'edge_type': jax.random.randint(ks[2], (E,), 0, R, jnp.int64), 'relation_emb': jax.random.normal(ks[3], (R, emb_dim), jnp.float32), 'msg_w': jax.random.normal(ks[4], (4, C, C), jnp.float32) * s, 'msg_b': jax.random.normal(ks[5], (4, C), jnp.float32) * s, 'upd_w': jax.random.normal(ks[6], (4, C, C), jnp.float32) * s, 'upd_b': jax.random.normal(ks[7], (4, C), jnp.float32) * s, 'gate_w': jax.random.normal(ks[8], (1, emb_dim), jnp.float32) * s, 'gate_b': jax.random.normal(ks[9], (1,), jnp.float32) * s}
    _L0_gnn_all = _L0_gnn_setup()
    _L0_gnn_in = {k: v for k, v in _L0_gnn_all.items() if k in ('relation_emb', 'msg_w', 'msg_b', 'upd_w', 'upd_b', 'gate_w', 'gate_b')}
    del _L0_gnn_all

    def _L1_gnn_setup():
        import jax, jax.numpy as jnp
        import numpy as np
        N_NODES = 1250
        N_EDGES = 40000
        D = 256

        def _mean_aggregate(x, src, dst, n_nodes):
            msg = x[src]
            summed = jax.ops.segment_sum(msg, dst, num_segments=n_nodes)
            deg = jax.ops.segment_sum(jnp.ones((src.shape[0],), x.dtype), dst, num_segments=n_nodes)
            return summed / jnp.maximum(deg, 1.0)[:, None]

        def _sage_conv(x, src, dst, Wl, bl, Wr, n_nodes):
            mean_nb = _mean_aggregate(x, src, dst, n_nodes)
            return mean_nb @ Wl.T + bl + x @ Wr.T
        key = jax.random.key(seed)
        ks = jax.random.split(key, 9)
        x = jax.random.normal(ks[0], (N_NODES, D), dtype=jnp.float32)
        edge_index = jax.random.randint(ks[1], (2, N_EDGES), 0, N_NODES, dtype=jnp.int32)
        s = 1.0 / np.sqrt(D)
        W1l = jax.random.uniform(ks[2], (D, D), jnp.float32, -s, s)
        b1l = jax.random.uniform(ks[3], (D,), jnp.float32, -s, s)
        W1r = jax.random.uniform(ks[4], (D, D), jnp.float32, -s, s)
        W2l = jax.random.uniform(ks[5], (D, D), jnp.float32, -s, s)
        b2l = jax.random.uniform(ks[6], (D,), jnp.float32, -s, s)
        W2r = jax.random.uniform(ks[7], (D, D), jnp.float32, -s, s)
        return {'x': x, 'edge_index': edge_index, 'W1l': W1l, 'b1l': b1l, 'W1r': W1r, 'W2l': W2l, 'b2l': b2l, 'W2r': W2r}
    _L1_gnn_all = _L1_gnn_setup()
    _L1_gnn_in = {k: v for k, v in _L1_gnn_all.items() if k in ('W1l', 'b1l', 'W1r', 'W2l', 'b2l', 'W2r')}
    del _L1_gnn_all
    return {'x': x, 'src': src, 'dst': dst, 'edge_type_500': edge_type_500, 'L0_gnn_relation_emb': _L0_gnn_in['relation_emb'], 'L0_gnn_msg_w': _L0_gnn_in['msg_w'], 'L0_gnn_msg_b': _L0_gnn_in['msg_b'], 'L0_gnn_upd_w': _L0_gnn_in['upd_w'], 'L0_gnn_upd_b': _L0_gnn_in['upd_b'], 'L0_gnn_gate_w': _L0_gnn_in['gate_w'], 'L0_gnn_gate_b': _L0_gnn_in['gate_b'], 'L1_gnn_W1l': _L1_gnn_in['W1l'], 'L1_gnn_b1l': _L1_gnn_in['b1l'], 'L1_gnn_W1r': _L1_gnn_in['W1r'], 'L1_gnn_W2l': _L1_gnn_in['W2l'], 'L1_gnn_b2l': _L1_gnn_in['b2l'], 'L1_gnn_W2r': _L1_gnn_in['W2r']}

def reference(x, src, dst, edge_type_500, L0_gnn_relation_emb, L0_gnn_msg_w, L0_gnn_msg_b, L0_gnn_upd_w, L0_gnn_upd_b, L0_gnn_gate_w, L0_gnn_gate_b, L1_gnn_W1l, L1_gnn_b1l, L1_gnn_W1r, L1_gnn_W2l, L1_gnn_b2l, L1_gnn_W2r):
    import jax
    import jax.numpy as jnp

    def _L0_gnn_ref(h, edge_index, edge_type, relation_emb, msg_w, msg_b, upd_w, upd_b, gate_w, gate_b):
        import jax, jax.numpy as jnp
        import numpy as np
        G = (1.0, 1.0)

        def to_hypercomplex(x, n_blades):
            return x.reshape(*x.shape[:-1], n_blades, -1).swapaxes(-2, -1)

        def clifford_kernel_2d(w, g):
            g0, g1 = g
            k0 = jnp.concatenate([w[0], g0 * w[1], g1 * w[2], -g0 * g1 * w[3]], axis=1)
            k1 = jnp.concatenate([w[1], w[0], -g1 * w[3], g1 * w[2]], axis=1)
            k2 = jnp.concatenate([w[2], g0 * w[3], w[0], -g0 * w[1]], axis=1)
            k3 = jnp.concatenate([w[3], w[2], w[1], w[0]], axis=1)
            return jnp.concatenate([k0, k1, k2, k3], axis=0)

        def clifford_linear(x, w, b, g=G):
            N = x.shape[0]
            k = clifford_kernel_2d(w, g)
            xf = x.swapaxes(-2, -1).reshape(N, -1)
            out = xf @ k.T + b.reshape(-1)
            C_out = w.shape[1]
            return out.reshape(N, 4, C_out).swapaxes(-2, -1)
        n_blades = 4
        num_nodes = h.shape[0]
        h_hc = to_hypercomplex(h, n_blades)
        r_hc = to_hypercomplex(relation_emb, n_blades)
        src, dst = (edge_index[0], edge_index[1])
        h_src = h_hc[src]
        r_uv = r_hc[edge_type]
        m = clifford_linear(h_src * r_uv, msg_w, msg_b)
        gate = jax.nn.sigmoid(r_uv.reshape(r_uv.shape[0], -1) @ gate_w.T + gate_b)
        m = m * gate[:, :, None]
        ones = jnp.ones_like(src, dtype=jnp.float32)
        deg_src = jax.ops.segment_sum(ones, src, num_segments=num_nodes)
        deg_dst = jax.ops.segment_sum(ones, dst, num_segments=num_nodes)
        norm = jnp.maximum(deg_src[src] * deg_dst[dst], 1.0) ** (-0.5)
        m = m * norm[:, None, None]
        h_agg = jax.ops.segment_sum(m, dst, num_segments=num_nodes)
        h_out = clifford_linear(h_hc + h_agg, upd_w, upd_b)
        return h_out.reshape(num_nodes, -1)

    def _L1_gnn_ref(x, edge_index, W1l, b1l, W1r, W2l, b2l, W2r):
        import jax, jax.numpy as jnp
        import numpy as np
        N_NODES = 1250
        N_EDGES = 40000
        D = 256

        def _mean_aggregate(x, src, dst, n_nodes):
            msg = x[src]
            summed = jax.ops.segment_sum(msg, dst, num_segments=n_nodes)
            deg = jax.ops.segment_sum(jnp.ones((src.shape[0],), x.dtype), dst, num_segments=n_nodes)
            return summed / jnp.maximum(deg, 1.0)[:, None]

        def _sage_conv(x, src, dst, Wl, bl, Wr, n_nodes):
            mean_nb = _mean_aggregate(x, src, dst, n_nodes)
            return mean_nb @ Wl.T + bl + x @ Wr.T
        src, dst = (edge_index[0], edge_index[1])
        n = x.shape[0]
        h = jax.nn.relu(_sage_conv(x, src, dst, W1l, b1l, W1r, n))
        h = jax.nn.relu(_sage_conv(h, src, dst, W2l, b2l, W2r, n))
        out = _sage_conv(h, src, dst, W2l, b2l, W2r, n)
        return out
    edge_index = jnp.stack([src, dst])
    x = _layernorm(x + _L0_gnn_ref(x, edge_index, edge_type_500, L0_gnn_relation_emb, L0_gnn_msg_w, L0_gnn_msg_b, L0_gnn_upd_w, L0_gnn_upd_b, L0_gnn_gate_w, L0_gnn_gate_b), axis=-1)
    x = _layernorm(x + _L1_gnn_ref(x, edge_index, L1_gnn_W1l, L1_gnn_b1l, L1_gnn_W1r, L1_gnn_W2l, L1_gnn_b2l, L1_gnn_W2r), axis=-1)
    return x

_drawn_inputs = setup_inputs


def setup_inputs(seed=0):
    import zlib

    import numpy as np

    out = dict(_drawn_inputs(seed))
    spreads = {}
    factors = {'L0_gnn_msg_b': 3.476, 'L0_gnn_gate_w': 2.702, 'L1_gnn_b1l': 7.056}
    for name, (base, spread) in spreads.items():
        noise = np.random.default_rng([zlib.crc32(name.encode()), seed]).standard_normal(out[name].shape)
        drawn = base * np.exp(spread * noise) if base else spread * noise
        out[name] = jnp.asarray(drawn.astype(out[name].dtype))
    for name, factor in factors.items():
        out[name] = (out[name] * factor).astype(out[name].dtype)
    return out
```

```python
from contextlib import ExitStack

import concourse.bass as bass
from concourse import mybir

F32 = mybir.dt.float32
BF16 = mybir.dt.bfloat16
F16 = mybir.dt.float16
I32 = mybir.dt.int32
ALU = mybir.AluOpType
ACT = mybir.ActivationFunctionType
AX_X = mybir.AxisListType.X

P = 128
WINDOW = 64
GC = 4
RING0, RING = 4, 8
HC = 8
HBUF = 3
LN_EPS = 1e-5
PAD_DST = 1000000
SETW = 33


def ceil_div(a, b):
    return (a + b - 1) // b


def gnn_program(nc, x, src, dst, typ, rel, msg_w, msg_b, upd_w, upd_b, gate_w, gate_b,
                W1l, b1l, W1r, W2l, b2l, W2r, out):
    N, D = x.shape
    E = src.shape[0]
    NREL = rel.shape[0]
    C = D // 4
    DH = D // P
    assert D == 256
    NB = ceil_div(N, P)
    NFULL = N // P
    NREM = N - NFULL * P
    NCH = ceil_div(E, P)
    EFULL = E // P
    EREM = E - EFULL * P
    NG = ceil_div(NCH, GC)
    EB = ceil_div(NG * GC, P)
    RK = next(k for k in range(ceil_div(NREL, P), NREL + 1) if NREL % k == 0)
    RP = NREL // RK
    ROUNDS = ceil_div(N, WINDOW)
    AGGW = NB * P + WINDOW
    TW = D + 4
    RW = D + 2
    assert N < PAD_DST and EB <= 8 and NB <= 128

    def chunks_of(g):
        return min(GC, NCH - GC * g)

    table0 = nc.dram_tensor("table_scaled_x", (N, TW), F32, kind="Internal").ap()
    tables = [nc.dram_tensor(f"table_h{k}", (N, D), F32, kind="Internal").ap() for k in (1, 2, 3)]

    with ExitStack() as ctx:
        def sem(name):
            return ctx.enter_context(nc.semaphore(name))

        def sb(name, shape, dt=F32, scope=None):
            return (scope or ctx).enter_context(nc.sbuf_tensor(name, shape, dt))

        bank = [ctx.enter_context(nc.psum_tensor(f"bank{i}", [P, 512], F32)) for i in range(8)]

        arena_w = {"raw": 3 * EB * P, "rawf": 2 * EB * P, "w_raw": 6 * DH * D, "blades": 8 * C, "rel_sb": RK * D,
                   "rel_f": RK * RW, "rel_rest": RK * RW}
        arena = sb("arena", [P, max(DH * AGGW, sum(arena_w.values()))])
        agg = arena[:, 0:DH * AGGW].rearrange("p (h n) -> p h n", h=DH)
        node_rows = sb("node_rows", [P, NB, D])
        src_idx = sb("src_idx", [P, EB * P], I32)
        dst_f = sb("dst_f", [P, EB * P])
        dst_local = sb("dst_local", [P, NG * GC])
        base0 = sb("base0", [P, NG])
        base_cur = sb("base_cur", [P, NG])
        base_int = sb("base_int", [1, NG], I32)
        base_step = sb("base_step", [P, 1])
        rounds_int = sb("rounds_int", [1, 1], I32)
        ident = sb("ident", [P, P])
        ones = sb("ones", [P, P])
        iota_w = sb("iota_w", [P, WINDOW])
        wT = {n: sb(f"wT_{n}", [P, DH, D]) for n in ("msg", "upd", "W1l", "W1r", "W2l", "W2r")}
        bias = {n: sb(f"bias_{n}", [P, D]) for n in ("msg", "upd", "b1l", "b2l")}
        rdeg = sb("rdeg", [P, NB])
        ddst = sb("ddst", [P, NB])
        s_sum = sb("s_sum", [P, NB])
        small = sb("small", [P, 8])

        pass0 = ExitStack()
        ctx.enter_context(pass0)
        rel_parts = sb("rel_parts", [RP, RK, 3, RW], BF16, pass0)
        type_id = sb("type_id", [RP, RK], F32, pass0)
        seg_row = sb("seg_row", [SETW, AGGW], F32, pass0)
        pick = sb("pick", [SETW, 2], F32, pass0)

        setup = ExitStack()
        def lent(name, rows=P):
            at = sum(w for n, w in list(arena_w.items())[:list(arena_w).index(name)])
            return arena[0:rows, at:at + arena_w[name]]

        raw = lent("raw").bitcast(I32).rearrange("p (a e) -> p a e", a=3)
        rawf = lent("rawf").rearrange("p (a e) -> p a e", a=2)
        idx_bits = sb("idx_bits", [P, 2, EB * P], I32, setup)
        idx_bf = sb("idx_bf", [P, 2, EB * P], BF16, setup)
        iota_b = sb("iota_b", [P, P], BF16, setup)
        lo_hot = sb("lo_hot", [P, HBUF, HC, P], BF16, setup)
        hi_hot = sb("hi_hot", [P, HBUF, HC, NB], BF16, setup)
        w_all = lent("w_raw").rearrange("p (n h i) -> p n h i", n=6, h=DH)
        w_raw = {n: w_all[:, i] for i, n in enumerate(("msg", "upd", "W1l", "W1r", "W2l", "W2r"))}
        blades = lent("blades").rearrange("p (a k i) -> p a k i", a=2, k=4)
        rel_sb = lent("rel_sb", RP).rearrange("p (k f) -> p k f", k=RK)
        rel_f = lent("rel_f", RP).rearrange("p (k f) -> p k f", k=RK)
        rel_rest = lent("rel_rest", RP).rearrange("p (k f) -> p k f", k=RK)
        gate_row = sb("gate_row", [RP, D], F32, setup)
        gate_bias = sb("gate_bias", [RP, 1], F32, setup)
        gate = sb("gate", [RP, 4, RK], F32, setup)
        dsrc = sb("dsrc", [P, 3, NB], F32, setup)
        outside = sb("outside", [P, 2, NG * GC], F32, setup)
        upd_turned = sb("upd_turned", [P, D], F32, setup)
        TS = 4
        staged = sb("staged", [P, 2, TS, TW], F32, setup)

        s_pads = sem("s_pads")
        s_edges = sem("s_edges")
        s_x = sem("s_x")
        s_w = sem("s_w")
        s_rel = sem("s_rel")
        s_const = sem("s_const")
        s_v = sem("s_v")
        s_rawf = sem("s_rawf")
        s_edgeT = sem("s_edgeT")
        s_edge_cp = sem("s_edge_cp")
        s_hot = sem("s_hot")
        s_hist = sem("s_hist")
        s_deg1 = sem("s_deg1")
        s_sqrt = sem("s_sqrt")
        s_exp_in = sem("s_exp_in")
        s_exp = sem("s_exp")
        s_K = sem("s_K")
        s_wT = sem("s_wT")
        s_wT_cp = sem("s_wT_cp")
        s_first = sem("s_first")
        s_lent = sem("s_lent")
        s_first_cp = sem("s_first_cp")
        s_viol = sem("s_viol")
        s_violT = sem("s_violT")
        s_stage = sem("s_stage")
        s_st_dma = [sem("s_st_dma0"), sem("s_st_dma1")]

        n_hist = ceil_div(NCH, HC)
        batches = [(b, min(TS, NB - b)) for b in range(0, NB, TS)]
        w_order = ["W1l", "W1r", "W2l", "W2r", "msg", "upd"]
        w_bank = dict(zip(w_order, (4, 5, 6, 4, 5, 6)))
        plain_w = {"W1l": W1l, "W1r": W1r, "W2l": W2l, "W2r": W2r}

        def rows_out(eng, table, tile, b0, n, signal):
            full = max(0, min(n, NFULL - b0))
            k = 0
            if full:
                eng.dma_start(table[b0 * P:(b0 + full) * P, :].rearrange("(b p) f -> p b f", p=P),
                              tile[:, 0:full, :]).then_inc(signal, 16)
                k += 1
            if full < n:
                eng.dma_start(table[NFULL * P:N, :], tile[0:NREM, full, :]).then_inc(signal, 16)
                k += 1
            return k

        def out_dmas(b0, n):
            full = max(0, min(n, NFULL - b0))
            return (1 if full else 0) + (1 if full < n else 0)

        with nc.Block() as block:
            @block.sync
            def _(sp):
                sp.wait_ge(s_pads, 4)
                for a, arr in enumerate((src, dst)):
                    full_blocks = EFULL // P
                    if full_blocks:
                        sp.dma_start(raw[:, a, 0:full_blocks * P].rearrange("p (b e) -> p b e", e=P),
                                     arr[0:full_blocks * P * P].rearrange("(b p e) -> p b e", p=P, e=P)
                                     ).then_inc(s_edges, 16)
                    more = EFULL - full_blocks * P
                    if more:
                        sp.dma_start(raw[0:more, a, full_blocks * P:(full_blocks + 1) * P],
                                     arr[full_blocks * P * P:EFULL * P].rearrange("(p e) -> p e", e=P)
                                     ).then_inc(s_edges, 16)
                    if EREM:
                        b = EFULL // P
                        sp.dma_start(raw[more:more + 1, a, b * P:b * P + EREM],
                                     arr[EFULL * P:E].rearrange("(a e) -> a e", a=1)).then_inc(s_edges, 16)
                for b in range(0, NFULL, 8):
                    n = min(8, NFULL - b)
                    sp.dma_start(node_rows[:, b:b + n, :],
                                 x[b * P:(b + n) * P, :].rearrange("(b p) f -> p b f", p=P)).then_inc(s_x, 16)
                if NREM:
                    sp.dma_start(node_rows[0:NREM, NB - 1, :], x[NFULL * P:N, :]).then_inc(s_x, 16)
                for i, (b, n) in enumerate(batches):
                    sp.wait_ge(s_stage, i + 1)
                    rows_out(sp, table0[:, :], staged[:, i % 2], b, n, s_st_dma[i % 2])
                for i in range(2):
                    sp.wait_ge(s_st_dma[i], 16 * sum(out_dmas(*batches[j]) for j in range(i, len(batches), 2)))

            n_edge_dmas = 2 * ((1 if EFULL // P else 0) + (1 if EFULL % P else 0) + (1 if EREM else 0))
            n_x_dmas = ceil_div(NFULL, 8) + (1 if NREM else 0)

            @block.scalar
            def _(act):
                act.dma_start(rel_sb[:], rel.rearrange("(k p) f -> p k f", p=RP)).then_inc(s_rel, 16)
                act.dma_start(gate_row[:], gate_w[0:1, :].to_broadcast([RP, D])).then_inc(s_rel, 16)
                act.dma_start(gate_bias[:], gate_b.rearrange("(a b) -> a b", a=1).to_broadcast([RP, 1])).then_inc(s_rel, 16)
                for n, w in plain_w.items():
                    act.dma_start(w_raw[n][:], w.rearrange("(h p) i -> p h i", p=P)).then_inc(s_w, 16)
                for h in range(2):
                    for a, w in enumerate((msg_w, upd_w)):
                        act.dma_start(blades[h * C:(h + 1) * C, a], w.rearrange("k o i -> o k i")).then_inc(s_w, 16)
                for n, v in (("msg", msg_b.rearrange("a c -> (a c)")), ("upd", upd_b.rearrange("a c -> (a c)")), ("b1l", b1l), ("b2l", b2l)):
                    act.dma_start(bias[n][:], v.rearrange("(a d) -> a d", a=1).to_broadcast([P, D])).then_inc(s_w, 16)
                act.wait_ge(s_exp_in, 1)
                act.activation(gate[:, 1, :], gate[:, 0, :], ACT.Exp, scale=-1.0).then_inc(s_exp, 1)
                for i, n in enumerate(w_order):
                    act.wait_ge(s_wT, i + 1)
                    ps = bank[w_bank[n]][:, :]
                    for ih in range(DH):
                        o = wT[n][:, ih, :]
                        v = ps[:, ih * D:(ih + 1) * D]
                        if n == "upd":
                            o = o.rearrange("p (c b) -> p b c", b=4)
                            v = v.rearrange("p (b c) -> p b c", b=4)
                        last = act.copy(o, v)
                    last.then_inc(s_wT_cp, 1)
                act.wait_ge(s_deg1, 1)
                act.activation(dsrc[:, 1, :], dsrc[:, 0, :], ACT.Sqrt).then_inc(s_sqrt, 1)

            n_w_dmas = 4 + 4 + 4

            @block.gpsimd
            def _(pool):
                pool.memset(ident[:], 0.0).then_inc(s_const, 1)
                pool.wait_ge(s_const, 1)
                pool.affine_select(out=ident[:], in_=ident[:], compare_op=ALU.not_equal, fill=1.0,
                                   base=0, pattern=[[-1, P]], channel_multiplier=1).then_inc(s_const, 1)
                pool.memset(ones[:], 1.0).then_inc(s_const, 1)
                pool.iota(iota_w[:], pattern=[[1, WINDOW]], base=0, channel_multiplier=0,
                          allow_small_or_imprecise_dtypes=True).then_inc(s_const, 1)
                pool.iota(iota_b[:], pattern=[[1, P]], base=0, channel_multiplier=0,
                          allow_small_or_imprecise_dtypes=True).then_inc(s_const, 1)
                pool.iota(type_id[:], pattern=[[RP, RK]], base=0, channel_multiplier=1,
                          allow_small_or_imprecise_dtypes=True).then_inc(s_const, 1)
                pool.memset(staged[:], 0.0).then_inc(s_const, 1)
                pool.memset(seg_row[:], 0.0).then_inc(s_const, 1)
                pool.memset(pick[:], 0.0).then_inc(s_const, 1)
                pool.wait_ge(s_const, 9)
                pool.memset(pick[0:1, 0:1], 1.0).then_inc(s_const, 1)
                pool.wait_ge(s_const, 10)
                pool.memset(pick[32:33, 1:2], 1.0).then_inc(s_const, 1)
                pool.wait_ge(s_const, 11)
                pool.wait_ge(s_wT, 6)
                pool.wait_ge(s_lent, 1)
                pool.memset(agg, 0.0).then_inc(s_const, 1)
                pool.wait_ge(s_const, 12)

            @block.vector
            def _(dve):
                done = [0]

                def step(ins):
                    done[0] += 1
                    ins.then_inc(s_v, 1)
                    dve.wait_ge(s_v, done[0])

                dve.memset(raw[:, 0, :], 0).then_inc(s_pads, 1)
                dve.memset(raw[:, 1, :], PAD_DST).then_inc(s_pads, 1)
                dve.memset(node_rows[:, NB - 1, :], 0.0).then_inc(s_pads, 1)
                dve.memset(outside[:], 0.0).then_inc(s_pads, 1)

                dve.wait_ge(s_edges, 16 * n_edge_dmas)
                dve.tensor_copy(rawf[:], raw[:, 0:2, :]).then_inc(s_rawf, 1)
                for a in range(2):
                    dve.wait_ge(s_edgeT, EB * (a + 1))
                    for b in range(EB):
                        v = bank[2 * a + b // 4][:, b % 4 * P:(b % 4 + 1) * P]
                        o = (src_idx if a == 0 else dst_f)[:, b * P:(b + 1) * P]
                        last = dve.tensor_copy(o, v)
                    step(last)
                    if a == 1:
                        dve.sem_inc(s_edge_cp, 1)
                    if a == 0:
                        dve.tensor_scalar(idx_bits[:, 0, :], src_idx[:], P - 1, None, ALU.bitwise_and)
                        step(dve.tensor_scalar(idx_bits[:, 1, :], src_idx[:], P.bit_length() - 1, None,
                                               ALU.logical_shift_right))
                        step(dve.tensor_copy(idx_bf[:], idx_bits[:]))

                dve.wait_ge(s_w, 16 * n_w_dmas)
                for a, n in enumerate(("msg", "upd")):
                    for i in range(4):
                        for j in range(4):
                            sign = -1.0 if (i, j) in ((0, 3), (1, 2), (2, 3)) else 1.0
                            h = slice(i % 2 * C, i % 2 * C + C)
                            last = dve.tensor_scalar(w_raw[n][h, i // 2, j * C:(j + 1) * C],
                                                     blades[h, a, i ^ j, :], sign, None, ALU.mult)
                    last.then_inc(s_K, 1)
                step(dve.tensor_copy(upd_turned[:, :].rearrange("p (c b) -> p c b", b=4),
                                     bias["upd"][:, :].rearrange("p (b c) -> p c b", b=4)))
                step(dve.tensor_copy(bias["upd"][:, :], upd_turned[:, :]))

                dve.wait_ge(s_rel, 48)
                dve.wait_ge(s_const, 9)
                step(dve.memset(rel_f[:, :, D + 1], 0.0))
                gate_by_blade = gate_row[:, :].rearrange("p (c b) -> p b c", b=4)
                for k in range(RK):
                    last = dve.tensor_tensor(rel_rest[:, k, 0:D].rearrange("p (b c) -> p b c", b=4),
                                             rel_sb[:, k, :].rearrange("p (b c) -> p b c", b=4),
                                             gate_by_blade, ALU.mult)
                step(last)
                step(dve.tensor_reduce(gate[:, 0, :], rel_rest[:, :, 0:D], AX_X, ALU.add))
                dve.tensor_scalar(gate[:, 0, :], gate[:, 0, :], gate_bias[:, 0:1], None, ALU.add).then_inc(s_exp_in, 1)
                dve.wait_ge(s_exp, 1)
                step(dve.tensor_scalar(gate[:, 2, :], gate[:, 1, :], 1.0, None, ALU.add))
                step(dve.reciprocal(gate[:, 3, :], gate[:, 2, :]))
                for k in range(RK):
                    dve.tensor_scalar(rel_f[:, k, 0:D], rel_sb[:, k, :], gate[:, 3, k:k + 1], None, ALU.mult)
                step(dve.tensor_copy(rel_f[:, :, D], gate[:, 3, :]))
                step(dve.tensor_copy(rel_parts[:, :, 0, :], rel_f[:]))
                step(dve.tensor_tensor(rel_rest[:], rel_f[:], rel_parts[:, :, 0, :], ALU.subtract))
                step(dve.tensor_copy(rel_parts[:, :, 1, :], rel_rest[:]))
                step(dve.tensor_tensor(rel_f[:], rel_rest[:], rel_parts[:, :, 1, :], ALU.subtract))
                step(dve.tensor_copy(rel_parts[:, :, 2, :], rel_f[:]))
                dve.sem_inc(s_lent, 1)

                dve.wait_ge(s_first, 1)
                step(dve.tensor_copy(base0[:], bank[7][:, 256:256 + NG]))
                dve.sem_inc(s_first_cp, 1)
                local = dst_local[:, :]
                step(dve.tensor_tensor(local.rearrange("p (g c) -> p g c", c=GC),
                                       dst_f[:, 0:NG * GC].rearrange("p (g c) -> p g c", c=GC),
                                       base0[:, :].unsqueeze(2).to_broadcast([P, NG, GC]), ALU.subtract))
                real = [(P, 0, EFULL)] + ([(EREM, EFULL, EFULL + 1)] if EREM else [])
                for rows, c0, c1 in real:
                    if c1 > c0:
                        dve.tensor_scalar(outside[0:rows, 0, c0:c1], local[0:rows, c0:c1], 0.0, None, ALU.is_lt)
                        step(dve.tensor_scalar(outside[0:rows, 1, c0:c1], local[0:rows, c0:c1],
                                               float(WINDOW - 1), None, ALU.is_gt))
                dve.tensor_reduce(small[:, 0:1], outside[:, :, :].rearrange("p a c -> p (a c)"), AX_X,
                                  ALU.add).then_inc(s_viol, 1)
                dve.wait_ge(s_violT, 1)
                step(dve.tensor_scalar(small[:, 1:2], bank[7][:, 510:511], 1.0, None, ALU.min))
                dve.tensor_scalar(rounds_int[:, :], small[0:1, 1:2], float(ROUNDS - 1), 1.0, ALU.mult, ALU.add)
                dve.tensor_scalar(base_step[:, :], small[:, 1:2], float(WINDOW), None, ALU.mult)
                step(dve.tensor_scalar(small[:, 2:3], small[:, 1:2], -1.0, 1.0, ALU.mult, ALU.add))
                step(dve.tensor_scalar(base0[:], base0[:], small[:, 2:3], None, ALU.mult))
                step(dve.tensor_copy(base_cur[:], base0[:]))

                for i in range(n_hist):
                    c0, n = i * HC, min(HC, NCH - i * HC)
                    if i >= HBUF:
                        dve.wait_ge(s_hist, i - HBUF + 1)
                    dve.tensor_tensor(lo_hot[:, i % HBUF, 0:n, :],
                                      iota_b[:, :].unsqueeze(1).to_broadcast([P, n, P]),
                                      idx_bf[:, 0, c0:c0 + n].unsqueeze(2).to_broadcast([P, n, P]),
                                      ALU.is_equal)
                    dve.tensor_tensor(hi_hot[:, i % HBUF, 0:n, :],
                                      iota_b[:, 0:NB].unsqueeze(1).to_broadcast([P, n, NB]),
                                      idx_bf[:, 1, c0:c0 + n].unsqueeze(2).to_broadcast([P, n, NB]),
                                      ALU.is_equal).then_inc(s_hot, 1)
                dve.wait_ge(s_hist, n_hist)
                dve.tensor_scalar(dsrc[:, 0, :], bank[7][:, 0:NB], 1.0, None, ALU.max).then_inc(s_deg1, 1)
                dve.wait_ge(s_sqrt, 1)
                step(dve.reciprocal(dsrc[:, 2, :], dsrc[:, 1, :]))
                dve.wait_ge(s_x, 16 * n_x_dmas)
                for i, (b0, n) in enumerate(batches):
                    if i >= 2:
                        dve.wait_ge(s_st_dma[i % 2], 16 * sum(out_dmas(*batches[j]) for j in range(i % 2, i, 2)))
                    for b in range(b0, b0 + n):
                        dve.tensor_scalar(staged[:, i % 2, b - b0, 0:D], node_rows[:, b, :],
                                          dsrc[:, 2, b:b + 1], None, ALU.mult)
                    dve.tensor_copy(staged[:, i % 2, 0:n, D], dsrc[:, 2, b0:b0 + n]).then_inc(s_stage, 1)

            @block.tensor
            def _(pe):
                pe.wait_ge(s_const, 9)
                pe.wait_ge(s_rawf, 1)
                for a in range(2):
                    for b in range(EB):
                        pe.transpose(bank[2 * a + b // 4][:, b % 4 * P:(b % 4 + 1) * P],
                                     rawf[:, a, b * P:(b + 1) * P], ident[:]).then_inc(s_edgeT, 1)
                pe.wait_ge(s_edge_cp, 1)
                pe.matmul(bank[7][:, 256:256 + NG], ones[0:1, :], dst_f[0:1, 0:NG * GC:GC],
                          start=True, stop=True).then_inc(s_first, 1)
                pe.wait_ge(s_w, 16 * n_w_dmas)
                for i, n in enumerate(w_order):
                    if n in ("msg", "upd"):
                        pe.wait_ge(s_K, 1 if n == "msg" else 2)
                    if i >= 3:
                        pe.wait_ge(s_wT_cp, i - 2)
                    for ih in range(DH):
                        for oh in range(DH):
                            last = pe.transpose(bank[w_bank[n]][:, ih * D + oh * P:ih * D + (oh + 1) * P],
                                                w_raw[n][:, oh, ih * P:(ih + 1) * P], ident[:])
                    last.then_inc(s_wT, 1)
                pe.wait_ge(s_viol, 1)
                pe.wait_ge(s_first_cp, 1)
                pe.matmul(bank[7][:, 510:511], ones[:, :], small[:, 0:1], start=True, stop=True).then_inc(s_violT, 1)
                for i in range(n_hist):
                    pe.wait_ge(s_hot, i + 1)
                    for c in range(i * HC, min(NCH, (i + 1) * HC)):
                        rows = P if c < EFULL else EREM
                        last = pe.matmul(bank[7][:, 0:NB], lo_hot[0:rows, i % HBUF, c - i * HC, :],
                                         hi_hot[0:rows, i % HBUF, c - i * HC, :], start=(c == 0), stop=(c == NCH - 1))
                    last.then_inc(s_hist, 1)
        setup.close()

        def edge_pass(k):
            first = k == 0
            ring = RING0 if first else RING
            table = table0 if first else tables[k - 1]
            width = TW if first else D
            with ExitStack() as tmp, ExitStack() as rctx:
                def lsem(name):
                    return rctx.enter_context(nc.semaphore(f"{name}_{k}"))

                rows = sb(f"rows{k}", [P, ring, GC, width], F32, tmp)
                hot = sb(f"hot{k}", [P, 2, GC, WINDOW], F32, tmp)
                s_rows = [lsem(f"s_rows{i}") for i in range(ring)]
                s_base = lsem("s_base")
                s_hot_d = lsem("s_hotd")
                s_seg = lsem("s_seg")
                s_add = lsem("s_add")
                s_free = lsem("s_free")
                pass_sems = s_rows + [s_base, s_hot_d, s_seg, s_add, s_free]
                if first:
                    types_i = sb("types_i", [RP, 2, GC * P], I32, tmp)
                    types_h = sb("types_h", [RP, 2, GC * P], F16, tmp)
                    type_hot = sb("type_hot", [RP, 2, RK, GC * P], BF16, tmp)
                    msg = sb("msg", [P, 2, GC, D + SETW], F32, tmp)
                    s_types = [lsem("s_types0"), lsem("s_types1")]
                    s_types_h = lsem("s_typesh")
                    s_type_hot = lsem("s_typehot")
                    s_rel_mm = lsem("s_relmm")
                    s_msg = lsem("s_msg")
                    s_init = lsem("s_init")
                    pass_sems += s_types + [s_types_h, s_type_hot, s_rel_mm, s_msg, s_init]
                else:
                    Wr, bl = ("W1r", "b1l") if k == 1 else ("W2r", "b2l")
                    HB = 3
                    h_in = sb(f"h_in{k}", [P, HB, D], F32, tmp)
                    hT = sb(f"hT{k}", [P, 2, DH, P], F32, tmp)
                    s_h = [lsem(f"s_h{i}") for i in range(HB)]
                    s_hT = lsem("s_hT")
                    s_hT_cp = lsem("s_hTcp")
                    s_z = lsem("s_z")
                    s_z_add = lsem("s_zadd")
                    pass_sems += s_h + [s_hT, s_hT_cp, s_z, s_z_add]
                    z_at = [[b for b in range(NB) if b * NG // NB == g] for g in range(NG)]

                def rows_full(g):
                    return 16 * sum(chunks_of(i) for i in range(g % ring, g + 1, ring))

                seg_bank = [bank[4], bank[5]]

                rounds = nc.values_load(rounds_int[0:1, 0:1], min_val=1, max_val=ROUNDS)
                with nc.Fori(0, rounds) as _round:
                    with nc.Block() as block:
                        @block.gpsimd
                        def _(pool):
                            for g in range(NG):
                                if g >= ring:
                                    pool.wait_ge(s_free, g - ring + 1)
                                for c in range(chunks_of(g)):
                                    col = g * GC + c
                                    pool.indirect_dma_start(
                                        out=rows[:, g % ring, c, :], out_offset=None, in_=table[:, :],
                                        in_offset=bass.IndirectOffsetOnAxis(ap=src_idx[:, col:col + 1], axis=0),
                                    ).then_inc(s_rows[g % ring], 16)

                        @block.sync
                        def _(sp):
                            if first:
                                sp.wait_ge(s_init, 1)
                                for g in range(NG):
                                    if g >= 2:
                                        sp.wait_ge(s_types_h, g - 1)
                                    n = min(GC * P, E - g * GC * P)
                                    sp.dma_start(types_i[:, g % 2, 0:n],
                                                 typ[g * GC * P:g * GC * P + n].rearrange("(a e) -> a e", a=1)
                                                 .to_broadcast([RP, n])).then_inc(s_types[g % 2], 16)
                            else:
                                for b in range(NB):
                                    if b >= HB:
                                        sp.wait_ge(s_hT, b - HB + 1)
                                    n = P if b < NFULL else NREM
                                    sp.dma_start(h_in[0:n, b % HB, :], table[b * P:b * P + n, :]
                                                 ).then_inc(s_h[b % HB], 16)

                        @block.scalar
                        def _(act):
                            if first:
                                for g in range(NG):
                                    act.wait_ge(s_types[g % 2], 16 * (g // 2 + 1))
                                    if g >= 2:
                                        act.wait_ge(s_type_hot, g - 1)
                                    act.copy(types_h[:, g % 2, :], types_i[:, g % 2, :]).then_inc(s_types_h, 1)
                            else:
                                for b in range(NB):
                                    act.wait_ge(s_hT, b + 1)
                                    if b >= 2:
                                        act.wait_ge(s_z, b - 1)
                                    act.copy(hT[:, b % 2, :, :].rearrange("p h n -> p (h n)"),
                                             bank[6][:, 0:D]).then_inc(s_hT_cp, 1)

                        @block.vector
                        def _(dve):
                            dve.tensor_tensor(dst_local[:, :].rearrange("p (g c) -> p g c", c=GC),
                                              dst_f[:, 0:NG * GC].rearrange("p (g c) -> p g c", c=GC),
                                              base_cur[:, :].unsqueeze(2).to_broadcast([P, NG, GC]),
                                              ALU.subtract).then_inc(s_base, 1)
                            dve.tensor_copy(base_int[:, :], base_cur[0:1, :]).then_inc(s_base, 1)
                            if first:
                                dve.memset(types_i[:], 0).then_inc(s_init, 1)
                                dve.memset(msg[:], 0.0).then_inc(s_base, 1)
                                dve.wait_ge(s_base, 3)
                                dve.memset(msg[:, :, :, D + SETW - 1], 1.0).then_inc(s_base, 1)
                            dve.wait_ge(s_base, 4 if first else 2)

                            def type_hots(g):
                                dve.wait_ge(s_types_h, g + 1)
                                if g >= 2:
                                    dve.wait_ge(s_rel_mm, GC * (g - 1))
                                for kk in range(RK):
                                    last = dve.tensor_scalar(type_hot[:, g % 2, kk, :], types_h[:, g % 2, :],
                                                             type_id[:, kk:kk + 1], None, ALU.is_equal)
                                last.then_inc(s_type_hot, 1)

                            def window_hots(g):
                                if g >= 2:
                                    dve.wait_ge(s_seg, g - 1)
                                dve.tensor_tensor(hot[:, g % 2, :, :],
                                                  iota_w[:, :].unsqueeze(1).to_broadcast([P, GC, WINDOW]),
                                                  dst_local[:, g * GC:(g + 1) * GC].unsqueeze(2)
                                                  .to_broadcast([P, GC, WINDOW]),
                                                  ALU.is_equal).then_inc(s_hot_d, 1)

                            def messages(g):
                                dve.wait_ge(s_rows[g % ring], rows_full(g))
                                if g >= 2:
                                    dve.wait_ge(s_seg, g - 1)
                                for c in range(chunks_of(g)):
                                    dve.wait_ge(s_rel_mm, GC * g + c + 1)
                                    last = dve.tensor_tensor(msg[:, g % 2, c, 0:D + 1], bank[c][:, 0:D + 1],
                                                             rows[:, g % ring, c, 0:D + 1], ALU.mult)
                                    last.then_inc(s_msg, 1)
                                dve.wait_ge(s_msg, GC * g + chunks_of(g))
                                dve.sem_inc(s_free, 1)

                            def add_window(g):
                                dve.wait_ge(s_seg, g + 1)
                                if g >= 1:
                                    dve.wait_ge(s_add, g)
                                at = dve.value_load(base_int[0:1, g:g + 1], min_val=0, max_val=N - 1)
                                ps = seg_bank[g % 2][:, 0:DH * WINDOW].rearrange("p (h w) -> p h w", h=DH)
                                if first:
                                    dst_row = seg_row[:, bass.ds(at, WINDOW)]
                                    dve.tensor_tensor(dst_row, dst_row,
                                                      seg_bank[g % 2][0:SETW, DH * WINDOW:(DH + 1) * WINDOW], ALU.add)
                                dst_cols = agg[:, :, bass.ds(at, WINDOW)]
                                dve.tensor_tensor(dst_cols, dst_cols, ps, ALU.add).then_inc(s_add, 1)

                            def z_add(b):
                                dve.wait_ge(s_z, b + 1)
                                dve.tensor_tensor(node_rows[:, b, :], bank[7][:, 0:D], bias[bl][:, :],
                                                  ALU.add).then_inc(s_z_add, 1)

                            if first:
                                type_hots(0)
                                for g in range(NG + 1):
                                    if g < NG:
                                        if g + 1 < NG:
                                            type_hots(g + 1)
                                        window_hots(g)
                                        messages(g)
                                    if g >= 1:
                                        add_window(g - 1)
                            else:
                                window_hots(0)
                                zb = 0
                                for g in range(NG):
                                    if g + 1 < NG:
                                        window_hots(g + 1)
                                    for b in z_at[g]:
                                        if b >= 1:
                                            z_add(b - 1)
                                    add_window(g)
                                z_add(NB - 1)
                            dve.wait_ge(s_add, NG)
                            dve.tensor_scalar(base_cur[:, :], base_cur[:, :], base_step[:, 0:1], None,
                                              ALU.add).then_inc(s_add, 1)
                            dve.wait_ge(s_add, NG + 1)

                        @block.tensor
                        def _(pe):
                            def relations(g):
                                pe.wait_ge(s_type_hot, g + 1)
                                for c in range(chunks_of(g)):
                                    if g >= 1:
                                        pe.wait_ge(s_msg, GC * (g - 1) + c + 1)
                                    for kk in range(RK):
                                        for part in range(3):
                                            last = pe.matmul(bank[c][:, 0:D + 1],
                                                             type_hot[:, g % 2, kk, c * P:(c + 1) * P],
                                                             rel_parts[:, kk, part, 0:D + 1],
                                                             start=(kk == 0 and part == 0),
                                                             stop=(kk == RK - 1 and part == 2))
                                    last.then_inc(s_rel_mm, 1)

                            def sums(g):
                                n = chunks_of(g)
                                pe.wait_ge(s_hot_d, g + 1)
                                if g >= 2:
                                    pe.wait_ge(s_add, g - 1)
                                if first:
                                    pe.wait_ge(s_msg, GC * g + n)
                                else:
                                    pe.wait_ge(s_rows[g % ring], rows_full(g))
                                data = msg[:, g % 2] if first else rows[:, g % ring]
                                for h in range(DH + first):
                                    lo, hi = (h * P, (h + 1) * P) if h < DH else (D, D + SETW)
                                    for c in range(n):
                                        last = pe.matmul(seg_bank[g % 2][0:hi - lo, h * WINDOW:(h + 1) * WINDOW],
                                                         data[:, c, lo:hi], hot[:, g % 2, c, :],
                                                         start=(c == 0), stop=(c == n - 1))
                                last.then_inc(s_seg, 1)
                                if not first:
                                    pe.wait_ge(s_seg, g + 1)
                                    pe.sem_inc(s_free, 1)

                            def z_turn(b):
                                n = P if b < NFULL else NREM
                                pe.wait_ge(s_h[b % HB], 16 * (b // HB + 1))
                                if b >= 1:
                                    pe.wait_ge(s_hT_cp, b)
                                for h in range(DH):
                                    last = pe.transpose(bank[6][:, h * P:h * P + n],
                                                        h_in[0:n, b % HB, h * P:(h + 1) * P], ident[0:n, 0:n])
                                last.then_inc(s_hT, 1)

                            def z_product(b):
                                pe.wait_ge(s_hT_cp, b + 1)
                                if b >= 1:
                                    pe.wait_ge(s_z_add, b)
                                for h in range(DH):
                                    last = pe.matmul(bank[7][:, 0:D], hT[:, b % 2, h, :], wT[Wr][:, h, :],
                                                     start=(h == 0), stop=(h == DH - 1))
                                last.then_inc(s_z, 1)

                            if first:
                                for g in range(NG + 1):
                                    if g < NG:
                                        relations(g)
                                    if g >= 1:
                                        sums(g - 1)
                            else:
                                for g in range(NG):
                                    for b in z_at[g]:
                                        z_turn(b)
                                        if b >= 1:
                                            z_product(b - 1)
                                    sums(g)
                                z_product(NB - 1)
                    for s in s_rows:
                        nc.gpsimd.dma_reset(range(s.num, s.num + 1))
                    for s in pass_sems:
                        nc.gpsimd.sem_clear(s)
                    nc.all_engine_barrier()

        BATCH = 4

        def node_stage(k):
            first, final = k == 0, k == 3
            Wl = ("msg", "W1l", "W2l", "W2l")[k]
            dest = out if final else tables[k]
            norm = first or final
            with ExitStack() as tmp:
                def lsem(name):
                    return ctx.enter_context(nc.semaphore(f"{name}_n{k}"))

                vec = sb(f"vec{k}", [P, 2, D], F32, tmp)
                vT = sb(f"vT{k}", [P, 2, D], F32, tmp)
                stats = sb(f"stats{k}", [P, 2, 6], F32, tmp)
                mv = sb(f"mv{k}", [P, NB, 2], F32, tmp)
                std = sb(f"std{k}", [P, 3, NB], F32, tmp)
                degs = sb(f"degs{k}", [P, 3, NB], F32, tmp)
                RB = 4
                x1_in = sb(f"x1_in{k}", [P, RB, D], F32, tmp)
                s_pick, s_deg, s_dsq = lsem("s_pick"), lsem("s_deg"), lsem("s_dsq")
                s_a, s_a_free = lsem("s_a"), lsem("s_afree")
                s_vec, s_vT, s_vT_cp, s_o, s_y = (lsem(n) for n in ("s_vec", "s_vT", "s_vTcp", "s_o", "s_y"))
                s_c, s_var, s_std, s_ready = (lsem(n) for n in ("s_c", "s_var", "s_std", "s_ready"))
                s_store = lsem("s_store")
                s_clear = lsem("s_clear")
                s_x1 = [lsem(f"s_x1{i}") for i in range(RB)] if final else []
                spans = [(b, min(BATCH, NB - b)) for b in range(0, NB, BATCH)]

                with nc.Block() as block:
                    @block.sync
                    def _(sp):
                        if final:
                            for b in range(NB):
                                if b >= RB:
                                    sp.wait_ge(s_y, b - RB + 1)
                                n = P if b < NFULL else NREM
                                sp.dma_start(x1_in[0:n, b % RB, :], tables[0][b * P:b * P + n, :]
                                             ).then_inc(s_x1[b % RB], 16)

                    @block.scalar
                    def _(act):
                        if first:
                            act.wait_ge(s_deg, 1)
                            act.activation(degs[:, 1, :], degs[:, 0, :], ACT.Sqrt).then_inc(s_dsq, 1)
                        st = 0
                        span_of = {b0 + n - 1: i for i, (b0, n) in enumerate(spans)}

                        def finish(i):
                            b0, n = spans[i]
                            if norm:
                                act.wait_ge(s_var, i + 1)
                                act.activation(std[:, 1, b0:b0 + n], std[:, 0, b0:b0 + n],
                                               ACT.Sqrt).then_inc(s_std, 1)

                        for b in range(NB):
                            if first:
                                act.wait_ge(s_vT, b + 1)
                                if b >= 2:
                                    act.wait_ge(s_o, b - 1)
                                act.copy(vT[:, b % 2, :], bank[2 + b % 2][:, 0:D]).then_inc(s_vT_cp, 1)
                            if not norm:
                                act.wait_ge(s_y, b + 1)
                                act.activation(node_rows[:, b, :], node_rows[:, b, :], ACT.Relu).then_inc(s_ready, 1)
                            if b in span_of:
                                finish(span_of[b])

                    @block.gpsimd
                    def _(pool):
                        total = 0
                        for i, (b0, n) in enumerate(spans):
                            if not final:
                                pool.wait_ge(s_a, b0 + n)
                                pool.memset(agg[:, :, b0 * P:(b0 + n) * P], 0.0).then_inc(s_clear, 1)
                            pool.wait_ge(s_ready, b0 + n)
                            total += rows_out(pool, dest, node_rows[:, b0:b0 + n], b0, n, s_store)
                        pool.wait_ge(s_store, 16 * total)
                        if not final:
                            pool.wait_ge(s_clear, len(spans))

                    @block.vector
                    def _(dve):
                        done = [0]

                        def step(ins):
                            track(ins)
                            dve.wait_ge(s_c, done[0])

                        def track(ins):
                            done[0] += 1
                            ins.then_inc(s_c, 1)

                        if first:
                            dve.wait_ge(s_pick, 1)
                            sd = bank[6][:, 0:2 * NB].rearrange("p (b t) -> p t b", t=2)
                            dve.tensor_copy(s_sum[:], sd[:, 0, :])
                            dve.tensor_scalar(degs[:, 0, :], sd[:, 1, :], 1.0, None, ALU.max).then_inc(s_deg, 1)
                            dve.wait_ge(s_deg, 1)
                            dve.reciprocal(rdeg[:], degs[:, 0, :])
                            dve.wait_ge(s_dsq, 1)
                            step(dve.reciprocal(ddst[:], degs[:, 1, :]))
                        step(dve.tensor_copy(base_cur[:], base0[:]))

                        def take(b):
                            dve.wait_ge(s_a, b + 1)
                            ps = bank[b % 2][:, 0:D]
                            if first:
                                if b >= 2:
                                    dve.wait_ge(s_vT, b - 1)
                                step(dve.scalar_tensor_tensor(out=vec[:, b % 2, :], in0=bias["msg"][:, :],
                                                              scalar=s_sum[:, b:b + 1], in1=ps,
                                                              op0=ALU.mult, op1=ALU.add))
                                dve.scalar_tensor_tensor(out=vec[:, b % 2, :], in0=vec[:, b % 2, :],
                                                         scalar=ddst[:, b:b + 1], in1=node_rows[:, b, :],
                                                         op0=ALU.mult, op1=ALU.add).then_inc(s_vec, 1)
                            else:
                                ins = dve.scalar_tensor_tensor(out=node_rows[:, b, :], in0=ps,
                                                               scalar=rdeg[:, b:b + 1], in1=node_rows[:, b, :],
                                                               op0=ALU.mult, op1=ALU.add)
                                if final:
                                    step(ins)
                                    dve.sem_inc(s_a_free, 1)
                                    dve.wait_ge(s_x1[b % RB], 16 * (b // RB + 1))
                                    n = P if b < NFULL else NREM
                                    step(dve.tensor_tensor(node_rows[0:n, b, :], node_rows[0:n, b, :],
                                                           x1_in[0:n, b % RB, :], ALU.add))
                                    dve.sem_inc(s_y, 1)
                                    moments(b)
                                else:
                                    ins.then_inc(s_y, 1)

                        def give(b):
                            dve.wait_ge(s_o, b + 1)
                            ps = bank[4 + b % 2][:, 0:D]
                            step(dve.tensor_tensor(node_rows[:, b, :], ps, node_rows[:, b, :], ALU.add))
                            dve.sem_inc(s_y, 1)
                            step(dve.tensor_tensor(node_rows[:, b, :], node_rows[:, b, :], bias["upd"][:, :], ALU.add))
                            moments(b)

                        def moments(b):
                            step(dve.bn_stats(stats[:, b % 2, :], node_rows[:, b, :]))
                            track(dve.bn_aggr(mv[:, b, :], stats[:, b % 2, :]))

                        def variance(i):
                            b0, n = spans[i]
                            dve.wait_ge(s_c, done[0])
                            step(dve.tensor_scalar(std[:, 0, b0:b0 + n], mv[:, b0:b0 + n, 1], LN_EPS, None, ALU.add))
                            dve.sem_inc(s_var, 1)

                        def normalise(i):
                            b0, n = spans[i]
                            dve.wait_ge(s_std, i + 1)
                            step(dve.reciprocal(std[:, 2, b0:b0 + n], std[:, 1, b0:b0 + n]))
                            for b in range(b0, b0 + n):
                                dve.tensor_scalar(node_rows[:, b, :], node_rows[:, b, :], mv[:, b, 0:1],
                                                  std[:, 2, b:b + 1], ALU.subtract, ALU.mult).then_inc(s_ready, 1)

                        if first:
                            pending = []
                            for b in range(NB + 2):
                                if b < NB:
                                    take(b)
                                if b >= 2:
                                    c = b - 2
                                    give(c)
                                    if pending:
                                        normalise(pending.pop())
                                    if c % BATCH == BATCH - 1 or c == NB - 1:
                                        variance(c // BATCH)
                                        pending.append(c // BATCH)
                            normalise(pending.pop())
                        elif final:
                            pending = []
                            for b in range(NB):
                                take(b)
                                if pending:
                                    normalise(pending.pop())
                                if b % BATCH == BATCH - 1 or b == NB - 1:
                                    variance(b // BATCH)
                                    pending.append(b // BATCH)
                            normalise(pending.pop())
                        else:
                            for b in range(NB):
                                take(b)

                    @block.tensor
                    def _(pe):
                        if first:
                            for b in range(NB):
                                last = pe.matmul(bank[6][:, 2 * b:2 * b + 2], seg_row[:, b * P:(b + 1) * P],
                                                 pick[:, :], start=True, stop=True)
                            last.then_inc(s_pick, 1)

                        def product(b):
                            if b >= 2:
                                pe.wait_ge(s_vec if first else (s_a_free if final else s_y), b - 1)
                            for h in range(DH):
                                last = pe.matmul(bank[b % 2][:, 0:D], agg[:, h, b * P:(b + 1) * P], wT[Wl][:, h, :],
                                                 start=(h == 0), stop=(h == DH - 1))
                            last.then_inc(s_a, 1)

                        def turn(b):
                            pe.wait_ge(s_vec, b + 1)
                            if b >= 2:
                                pe.wait_ge(s_vT_cp, b - 1)
                            for h in range(DH):
                                last = pe.transpose(bank[2 + b % 2][:, h * P:(h + 1) * P],
                                                    vec[:, b % 2, h * P:(h + 1) * P], ident[:])
                            last.then_inc(s_vT, 1)

                        def update(b):
                            pe.wait_ge(s_vT_cp, b + 1)
                            if b >= 2:
                                pe.wait_ge(s_y, b - 1)
                            for h in range(DH):
                                last = pe.matmul(bank[4 + b % 2][:, 0:D], vT[:, b % 2, h * P:(h + 1) * P],
                                                 wT["upd"][:, h, :], start=(h == 0), stop=(h == DH - 1))
                            last.then_inc(s_o, 1)

                        if first:
                            for b in range(NB + 2):
                                if b < NB:
                                    product(b)
                                if 1 <= b <= NB:
                                    turn(b - 1)
                                if b >= 2:
                                    update(b - 2)
                        else:
                            for b in range(NB):
                                product(b)

        for k in range(4):
            edge_pass(k)
            node_stage(k)
            if k == 0:
                pass0.close()


_INS = ["x", "src", "dst", "edge_type_500", "L0_gnn_relation_emb", "L0_gnn_msg_w", "L0_gnn_msg_b", "L0_gnn_upd_w",
        "L0_gnn_upd_b", "L0_gnn_gate_w", "L0_gnn_gate_b", "L1_gnn_W1l", "L1_gnn_b1l", "L1_gnn_W1r", "L1_gnn_W2l",
        "L1_gnn_b2l", "L1_gnn_W2r"]


def kernel(**inputs):
    import numpy as _np
    import concourse.bacc as _bacc
    from concourse import mybir as _mybir
    from concourse.bass_utils import run_bass_kernel_spmd as _run

    nc = _bacc.Bacc("TRN2", target_bir_lowering=False, num_devices=1)
    arrays, args = {}, []
    for name in _INS:
        a = _np.ascontiguousarray(inputs[name])
        arrays[f"in_{name}_dram"] = a
        args.append(nc.dram_tensor(f"in_{name}_dram", a.shape, _mybir.dt.from_np(a.dtype), kind="ExternalInput").ap())
    out = nc.dram_tensor("out_0_dram", inputs["x"].shape, _mybir.dt.float32, kind="ExternalOutput").ap()
    gnn_program(nc, *args, out)
    r = _run(nc, [arrays], core_ids=[0])
    return r.results[0]["out_0_dram"]
```

```python
from contextlib import ExitStack

import concourse.bass as bass
from concourse import mybir

F32 = mybir.dt.float32
BF16 = mybir.dt.bfloat16
F16 = mybir.dt.float16
I32 = mybir.dt.int32
ALU = mybir.AluOpType
ACT = mybir.ActivationFunctionType
AX_X = mybir.AxisListType.X

P = 128
WINDOW = 48
GC = 4
TYPES = 3
POOL_REL = ((0, 1),)
RING0, RING = 4, 4
SG = 4
DW = 3
CHUNK_W = 16
HBATCH = 4
HTILE = 4
ATILES = 2
EARLY = 10
COUNT_BUFS = 3
HC = 8
HBUF = 3
LN_EPS = 1e-5
PAD_DST = 1000000
SETW = 33


def ceil_div(a, b):
    return (a + b - 1) // b


def gnn_program(nc, x, src, dst, typ, rel, msg_w, msg_b, upd_w, upd_b, gate_w, gate_b,
                W1l, b1l, W1r, W2l, b2l, W2r, out):
    N, D = x.shape
    E = src.shape[0]
    NREL = rel.shape[0]
    C = D // 4
    DH = D // P
    assert D == 256
    NB = ceil_div(N, P)
    NFULL = N // P
    NREM = N - NFULL * P
    NCH = ceil_div(E, P)
    EFULL = E // P
    EREM = E - EFULL * P
    NG = ceil_div(NCH, GC)
    EB = ceil_div(NG * GC, P)
    RK = next(k for k in range(ceil_div(NREL, P), NREL + 1) if NREL % k == 0)
    RP = NREL // RK
    ROUNDS = ceil_div(N, WINDOW)
    WD = max(1, round(0.25 * NG / (SG * DW)))
    G0 = NG - WD * DW * SG
    C0 = G0 * GC
    ND = NCH - C0
    NDP = NG * GC - C0
    SGC = SG * GC
    SGW = 8 * ceil_div(int(SGC * P * N / E) + 24, 8)
    HH = ceil_div(NB, 2)
    TPW = ceil_div(NB, HTILE)
    assert G0 > 0 and DW * SGW <= 512 and HH * CHUNK_W <= 512 and NG + NDP <= 508
    AGGW = NB * P + max(WINDOW, SGW)
    TW = D + 4
    RW = D + 2
    assert N < PAD_DST and EB <= 8 and NB <= 128

    SLOPE = GC * P * N / E
    SLACK = ceil_div(3 * int(E ** 0.5) * N, E)
    def first_dst_at_least(g):
        return int(SLOPE * g - SLACK) - 1

    def dst_below(g):
        return int(SLOPE * g + SLACK) + 2 + WINDOW

    def chunks_of(g):
        return min(GC, NCH - GC * g)

    table0 = nc.dram_tensor("table_scaled_x", (N, TW), F32, kind="Internal").ap()
    table_rel = nc.dram_tensor("table_relations", (NREL, RW), F32, kind="Internal").ap()
    counts = nc.dram_tensor("edge_counts", (WD * DW, P, NB, SGW), BF16, kind="Internal").ap()
    tables = [nc.dram_tensor(f"table_h{k}", (N, D), F32, kind="Internal").ap() for k in (1, 2, 3)]

    with ExitStack() as ctx:
        def sem(name):
            return ctx.enter_context(nc.semaphore(name))

        def sb(name, shape, dt=F32, scope=None):
            return (scope or ctx).enter_context(nc.sbuf_tensor(name, shape, dt))

        bank = [ctx.enter_context(nc.psum_tensor(f"bank{i}", [P, 512], F32)) for i in range(8)]

        arena_w = {"raw": 3 * EB * P, "rawf": 3 * EB * P, "w_raw": 6 * DH * D, "blades": 8 * C, "rel_sb": RK * D,
                   "rel_f": RK * RW, "rel_rest": 2 * RK * RW}
        arena = sb("arena", [P, max(DH * AGGW, sum(arena_w.values()))])
        agg = arena[:, 0:DH * AGGW].rearrange("p (h n) -> p h n", h=DH)
        pass0_w = {"rows": RING0 * GC * TW, "msg": 2 * GC * (D + SETW), "rel_rows": RING0 * max(map(len, POOL_REL)) * RW,
                   "types_i": TYPES * GC * P, "types_h": GC * P, "type_hot": RK * GC * P}
        split_w = {"parts": NB * 3 * D // 2, "h_batch": 2 * HBATCH * D}
        row_w = {"block_rows": max(NB * TW, sum(pass0_w.values())), "rel_parts": RK * 3 * RW // 2, "seg_row": AGGW}
        rows_arena = sb("rows_arena", [P, max(sum(row_w.values()), sum(split_w.values()))])
        x_rows = rows_arena[:, 0:NB * TW].rearrange("p (b f) -> p b f", f=TW)
        node_rows = rows_arena[:, 0:NB * D].rearrange("p (b f) -> p b f", f=D)

        def lent_rows(name, rows=P, widths=pass0_w):
            at = sum(w for n, w in list(widths.items())[:list(widths).index(name)])
            return rows_arena[0:rows, at:at + widths[name]]

        type_idx = sb("type_idx", [P, EB * P], I32)
        src_idx = sb("src_idx", [P, EB * P], I32)
        dst_f = sb("dst_f", [P, EB * P])
        dst_local = sb("dst_local", [P, NG * GC])
        base0 = sb("base0", [P, NG])
        base_cur = sb("base_cur", [P, NG])
        base_int = sb("base_int", [1, NG], I32)
        base_step = sb("base_step", [P, 1])
        rounds_int = sb("rounds_int", [1, 1], I32)
        ident = sb("ident", [P, P])
        ones = sb("ones", [P, P])
        iota_w = sb("iota_w", [P, WINDOW])
        wT = {n: sb(f"wT_{n}", [P, DH, D]) for n in ("msg", "upd", "W1l", "W1r", "W2l", "W2r")}
        bias = {n: sb(f"bias_{n}", [P, D]) for n in ("msg", "upd", "b1l", "b2l")}
        rdeg = sb("rdeg", [P, NB])
        ddst = sb("ddst", [P, NB])
        s_sum = sb("s_sum", [P, NB])
        small = sb("small", [P, 8])
        src_lo = sb("src_lo", [P, NDP])
        src_dst_key = sb("src_dst_key", [P, NDP])
        chunk_at = sb("chunk_at", [1, NDP], I32)
        iota_key = sb("iota_key", [P, NB * CHUNK_W], F16)
        iota_b = sb("iota_b", [P, P], BF16)

        pass0 = ExitStack()
        ctx.enter_context(pass0)
        rel_parts = (lent_rows("rel_parts", RP, row_w).bitcast(BF16)
                     .rearrange("p (k a f) -> p k a f", k=RK, a=3))
        type_id = sb("type_id", [RP, RK], F32, pass0)
        seg_row = lent_rows("seg_row", SETW, row_w)
        pick = sb("pick", [SETW, 2], F32, pass0)

        setup = ExitStack()
        def lent(name, rows=P):
            at = sum(w for n, w in list(arena_w.items())[:list(arena_w).index(name)])
            return arena[0:rows, at:at + arena_w[name]]

        raw = lent("raw").bitcast(I32).rearrange("p (a e) -> p a e", a=3)
        rawf = lent("rawf").rearrange("p (a e) -> p a e", a=3)
        idx_bits = sb("idx_bits", [P, 2, EB * P], I32, setup)
        idx_f = sb("idx_f", [P, 2, EB * P], F32, setup)
        idx_h = sb("idx_h", [P, 2, EB * P], BF16, setup)
        check_w = {"iota_key": NB * CHUNK_W, "chunk_out": 2 * NDP, "outside": 2 * NG * GC}
        assert sum(check_w.values()) <= AGGW
        check = lent_rows("seg_row", P, row_w)
        iota_key_f = check[:, 0:check_w["iota_key"]]
        chunk_out = check[:, check_w["iota_key"]:][:, 0:check_w["chunk_out"]].rearrange("p (a c) -> p a c", a=2)
        outside = (check[:, check_w["iota_key"] + check_w["chunk_out"]:][:, 0:check_w["outside"]]
                   .rearrange("p (a c) -> p a c", a=2))
        chunk_first = sb("chunk_first", [P, NDP], F32, setup)
        chunk_row = sb("chunk_row", [1, 2, NDP], F32, setup)
        iota_rep = sb("iota_rep", [P, P, HC], BF16, setup)
        lo_hot = sb("lo_hot", [P, HBUF, P, HC], BF16, setup)
        hi_hot = sb("hi_hot", [P, HBUF, NB, HC], BF16, setup)
        w_all = lent("w_raw").rearrange("p (n h i) -> p n h i", n=6, h=DH)
        w_raw = {n: w_all[:, i] for i, n in enumerate(("msg", "upd", "W1l", "W1r", "W2l", "W2r"))}
        blades = lent("blades").rearrange("p (a k i) -> p a k i", a=2, k=4)
        rel_sb = lent("rel_sb", RP).rearrange("p (k f) -> p k f", k=RK)
        rel_f = lent("rel_f", RP).rearrange("p (k f) -> p k f", k=RK)
        rel_rest, rel_rest2 = (lent("rel_rest", RP)[:, i * RK * RW:(i + 1) * RK * RW].rearrange("p (k f) -> p k f", k=RK)
                               for i in range(2))
        gate_row = sb("gate_row", [RP, D], F32, setup)
        gate_bias = sb("gate_bias", [RP, 1], F32, setup)
        gate = sb("gate", [RP, 4, RK], F32, setup)
        dsrc = sb("dsrc", [P, 3, NB], F32, setup)
        upd_turned = sb("upd_turned", [P, D], F32, setup)
        TS = 7
        least = sb("least", [1, 3, NG], F32, setup)

        s_pads = sem("s_pads")
        s_x_pad = sem("s_x_pad")
        s_edges = [sem(f"s_edges{i}") for i in range(3)]
        s_x = sem("s_x")
        s_w = sem("s_w")
        s_rel = sem("s_rel")
        s_const = sem("s_const")
        s_v = sem("s_v")
        s_pool = sem("s_pool")
        s_rawf = [sem(f"s_rawf{i}") for i in range(3)]
        s_edgeT = [sem(f"s_edgeT{i}") for i in range(3)]
        s_dst_cp = sem("s_dst_cp")
        s_type_cp = sem("s_type_cp")
        s_hot = sem("s_hot")
        s_hist = sem("s_hist")
        s_deg1 = sem("s_deg1")
        s_sqrt = sem("s_sqrt")
        s_gate_in = sem("s_gate_in")
        s_logit = sem("s_logit")
        s_exp = sem("s_exp")
        s_gate = sem("s_gate")
        s_K = sem("s_K")
        s_wT = sem("s_wT")
        s_wT_cp = sem("s_wT_cp")
        s_first = sem("s_first")
        s_first_cp = sem("s_first_cp")
        s_viol = sem("s_viol")
        s_violT = sem("s_violT")
        s_scaled = sem("s_scaled")
        s_rel_f = sem("s_rel_f")
        s_tab = sem("s_tab")
        s_rel_tab = sem("s_rel_tab")

        n_hist = ceil_div(NCH, HC)
        batches = [(b, min(TS, NB - b)) for b in range(0, NB, TS)]
        w_order = ["W1l", "W1r", "W2l", "W2r", "msg", "upd"]
        turned_bank = bank[6]
        plain_w = {"W1l": W1l, "W1r": W1r, "W2l": W2l, "W2r": W2r}
        at_turn_edges, at_turn_w, at_first, at_viol = (min(n_hist - 1, i) for i in (2, 4, 12, 24))

        def rows_out(eng, table, tile, b0, n, signal):
            full = max(0, min(n, NFULL - b0))
            k = 0
            if full:
                eng.dma_start(table[b0 * P:(b0 + full) * P, :].rearrange("(b p) f -> p b f", p=P),
                              tile[:, 0:full, :]).then_inc(signal, 16)
                k += 1
            if full < n:
                eng.dma_start(table[NFULL * P:N, :], tile[0:NREM, full, :]).then_inc(signal, 16)
                k += 1
            return k

        def out_dmas(b0, n):
            full = max(0, min(n, NFULL - b0))
            return (1 if full else 0) + (1 if full < n else 0)

        def load_edges(eng, a, arr):
            full_blocks = EFULL // P
            if full_blocks:
                eng.dma_start(raw[:, a, 0:full_blocks * P].rearrange("p (b e) -> p b e", e=P),
                              arr[0:full_blocks * P * P].rearrange("(b p e) -> p b e", p=P, e=P)
                              ).then_inc(s_edges[a], 16)
            more = EFULL - full_blocks * P
            if more:
                eng.dma_start(raw[0:more, a, full_blocks * P:(full_blocks + 1) * P],
                              arr[full_blocks * P * P:EFULL * P].rearrange("(p e) -> p e", e=P)
                              ).then_inc(s_edges[a], 16)
            if EREM:
                b = EFULL // P
                eng.dma_start(raw[more:more + 1, a, b * P:b * P + EREM],
                              arr[EFULL * P:E].rearrange("(a e) -> a e", a=1)).then_inc(s_edges[a], 16)

        n_edge_dmas = (1 if EFULL // P else 0) + (1 if EFULL % P else 0) + (1 if EREM else 0)
        n_x_dmas = ceil_div(NFULL, 8) + (1 if NREM else 0)
        n_w_dmas = 4 + 4 + 4

        with nc.Block() as block:
            @block.sync
            def _(sp):
                sp.wait_ge(s_pads, 3)
                load_edges(sp, 0, src)
                load_edges(sp, 1, dst)
                load_edges(sp, 2, typ)
                sp.wait_ge(s_x_pad, 1)
                for b in range(0, NFULL, 8):
                    n = min(8, NFULL - b)
                    sp.dma_start(x_rows[:, b:b + n, 0:D],
                                 x[b * P:(b + n) * P, :].rearrange("(b p) f -> p b f", p=P)).then_inc(s_x, 16)
                if NREM:
                    sp.dma_start(x_rows[0:NREM, NB - 1, 0:D], x[NFULL * P:N, :]).then_inc(s_x, 16)
                sp.wait_ge(s_rel_f, 1)
                sp.dma_start(table_rel.rearrange("(k p) f -> p k f", p=RP), rel_f).then_inc(s_rel_tab, 16)
                for i, (b, n) in enumerate(batches):
                    sp.wait_ge(s_scaled, i + 1)
                    rows_out(sp, table0[:, :], x_rows[:, b:b + n], b, n, s_tab)
                sp.wait_ge(s_tab, 16 * sum(out_dmas(*i) for i in batches))

            @block.scalar
            def _(act):
                act.dma_start(rel_sb, rel.rearrange("(k p) f -> p k f", p=RP)).then_inc(s_rel, 16)
                act.dma_start(gate_row[:], gate_w[0:1, :].to_broadcast([RP, D])).then_inc(s_rel, 16)
                act.dma_start(gate_bias[:], gate_b.rearrange("(a b) -> a b", a=1).to_broadcast([RP, 1])).then_inc(s_rel, 16)
                for h in range(2):
                    for a, w in enumerate((msg_w, upd_w)):
                        act.dma_start(blades[h * C:(h + 1) * C, a], w.rearrange("k o i -> o k i")).then_inc(s_w, 16)
                for n, w in plain_w.items():
                    act.dma_start(w_raw[n], w.rearrange("(h p) i -> p h i", p=P)).then_inc(s_w, 16)
                for n, v in (("msg", msg_b.rearrange("a c -> (a c)")), ("upd", upd_b.rearrange("a c -> (a c)")), ("b1l", b1l), ("b2l", b2l)):
                    act.dma_start(bias[n][:], v.rearrange("(a d) -> a d", a=1).to_broadcast([P, D])).then_inc(s_w, 16)
                for a in (1, 2):
                    act.wait_ge(s_edges[a], 16 * n_edge_dmas)
                    act.copy(rawf[:, a, :], raw[:, a, :]).then_inc(s_rawf[a], 1)
                for a in (1, 2):
                    act.wait_ge(s_edgeT[a], EB)
                    for b in range(0, EB, 4):
                        n = min(4, EB - b) * P
                        last = act.copy((dst_f if a == 1 else type_idx)[:, b * P:b * P + n],
                                        bank[2 * a + b // 4][:, 0:n])
                    last.then_inc(s_dst_cp if a == 1 else s_type_cp, 1)
                for i, n in enumerate(w_order):
                    act.wait_ge(s_wT, i + 1)
                    ps = turned_bank[:, :]
                    for ih in range(DH):
                        o = wT[n][:, ih, :]
                        v = ps[:, ih * D:(ih + 1) * D]
                        if n == "upd":
                            o = o.rearrange("p (c b) -> p b c", b=4)
                            v = v.rearrange("p (b c) -> p b c", b=4)
                        last = act.copy(o, v)
                    last.then_inc(s_wT_cp, 1)
                act.wait_ge(s_logit, 1)
                act.activation(gate[:, 1, :], gate[:, 0, :], ACT.Exp, scale=-1.0).then_inc(s_exp, 1)
                act.wait_ge(s_deg1, 1)
                act.activation(dsrc[:, 1, :], dsrc[:, 0, :], ACT.Sqrt).then_inc(s_sqrt, 1)

            @block.gpsimd
            def _(pool):
                done = [0]

                def step(ins):
                    done[0] += 1
                    ins.then_inc(s_pool, 1)
                    pool.wait_ge(s_pool, done[0])

                pool.memset(x_rows[:, NB - 1, :], 0.0).then_inc(s_x_pad, 1)
                step(pool.memset(ident[:], 0.0))
                step(pool.affine_select(out=ident[:], in_=ident[:], compare_op=ALU.not_equal, fill=1.0,
                                        base=0, pattern=[[-1, P]], channel_multiplier=1))
                pool.memset(ones[:], 1.0).then_inc(s_const, 1)
                pool.iota(iota_b[:], pattern=[[1, P]], base=0, channel_multiplier=0,
                          allow_small_or_imprecise_dtypes=True).then_inc(s_const, 1)
                pool.iota(iota_key_f, pattern=[[1, NB * CHUNK_W]], base=0, channel_multiplier=0,
                          allow_small_or_imprecise_dtypes=True).then_inc(s_const, 1)
                pool.iota(iota_w[:], pattern=[[1, WINDOW]], base=0, channel_multiplier=0,
                          allow_small_or_imprecise_dtypes=True).then_inc(s_const, 1)
                pool.iota(type_id[:], pattern=[[RP, RK]], base=0, channel_multiplier=1,
                          allow_small_or_imprecise_dtypes=True).then_inc(s_const, 1)
                pool.iota(least[:, 0, :], pattern=[[1, NG]], base=0, channel_multiplier=0,
                          allow_small_or_imprecise_dtypes=True).then_inc(s_const, 1)
                pool.wait_ge(s_w, 16 * n_w_dmas)
                for a, n in enumerate(("msg", "upd")):
                    for i in range(4):
                        for j in range(4):
                            sign = -1.0 if (i, j) in ((0, 3), (1, 2), (2, 3)) else 1.0
                            h = slice(i % 2 * C, i % 2 * C + C)
                            last = pool.tensor_scalar(w_raw[n][h, i // 2, j * C:(j + 1) * C],
                                                      blades[h, a, i ^ j, :], sign, None, ALU.mult)
                            step(last)
                    pool.sem_inc(s_K, 1)
                step(pool.tensor_copy(upd_turned[:, :].rearrange("p (c b) -> p b c", b=4),
                                      bias["upd"][:, :].rearrange("p (b c) -> p b c", b=4)))
                step(pool.tensor_copy(bias["upd"][:, :], upd_turned[:, :]))
                pool.wait_ge(s_rel, 48)
                gate_by_blade = gate_row[:, :].rearrange("p (c b) -> p b c", b=4)
                step(pool.memset(rel_f[:, :, D + 1], 0.0))
                for k in range(RK):
                    step(pool.tensor_tensor(rel_rest[:, k, 0:D].rearrange("p (b c) -> p b c", b=4),
                                            rel_sb[:, k, :].rearrange("p (b c) -> p b c", b=4),
                                            gate_by_blade, ALU.mult))
                pool.sem_inc(s_gate_in, 1)
                pool.wait_ge(s_gate, 1)
                for k in range(RK):
                    step(pool.tensor_scalar(rel_f[:, k, 0:D], rel_sb[:, k, :], gate[:, 3, k:k + 1], None, ALU.mult))
                step(pool.tensor_copy(rel_f[:, :, D], gate[:, 3, :]))
                pool.sem_inc(s_rel_f, 1)
                step(pool.tensor_copy(rel_parts[:, :, 0, :], rel_f))
                step(pool.tensor_tensor(rel_rest, rel_f, rel_parts[:, :, 0, :], ALU.subtract))
                step(pool.tensor_copy(rel_parts[:, :, 1, :], rel_rest))
                step(pool.tensor_tensor(rel_rest2, rel_rest, rel_parts[:, :, 1, :], ALU.subtract))
                step(pool.tensor_copy(rel_parts[:, :, 2, :], rel_rest2))
                pool.wait_ge(s_viol, 2)
                step(pool.memset(seg_row, 0.0))
                step(pool.memset(pick[:], 0.0))
                step(pool.memset(pick[0:1, 0:1], 1.0))
                step(pool.memset(pick[32:33, 1:2], 1.0))
                pool.wait_ge(s_wT, 6)
                pool.wait_ge(s_edgeT[2], EB)
                pool.wait_ge(s_rel_tab, 16)
                step(pool.memset(agg, 0.0))

            @block.vector
            def _(dve):
                done = [0]

                def step(ins):
                    done[0] += 1
                    ins.then_inc(s_v, 1)
                    dve.wait_ge(s_v, done[0])

                dve.memset(raw[:, 0, :], 0).then_inc(s_pads, 1)
                dve.memset(raw[:, 1, :], PAD_DST).then_inc(s_pads, 1)
                dve.memset(raw[:, 2, :], 0).then_inc(s_pads, 1)
                dve.memset(chunk_out, 0.0)
                dve.memset(chunk_row[:], 0.0)
                dve.memset(outside, 0.0).then_inc(s_viol, 1)
                dve.wait_ge(s_edges[0], 16 * n_edge_dmas)
                dve.tensor_copy(rawf[:, 0, :], raw[:, 0, :]).then_inc(s_rawf[0], 1)
                dve.wait_ge(s_edgeT[0], EB)
                for b in range(0, EB, 4):
                    n = min(4, EB - b) * P
                    last = dve.tensor_copy(src_idx[:, b * P:b * P + n], bank[b // 4][:, 0:n])
                step(last)
                dve.tensor_scalar(idx_bits[:, 0, :], src_idx[:], P - 1, None, ALU.bitwise_and)
                step(dve.tensor_scalar(idx_bits[:, 1, :], src_idx[:], P.bit_length() - 1, None,
                                       ALU.logical_shift_right))
                dve.tensor_copy(idx_h[:], idx_bits[:])
                step(dve.tensor_copy(idx_f[:], idx_bits[:]))

                def window_base():
                    dve.wait_ge(s_first, 1)
                    step(dve.tensor_copy(base0[:], bank[6][:, 0:NG]))
                    step(dve.tensor_copy(chunk_first[:], bank[6][:, NG:NG + NDP]))
                    step(dve.tensor_copy(iota_key[:], iota_key_f))
                    dve.sem_inc(s_first_cp, 1)
                    step(dve.tensor_scalar(least[:, 1, :], least[:, 0, :], SLOPE, -float(SLACK), ALU.mult, ALU.add))
                    step(dve.tensor_scalar(least[:, 2, :], least[:, 1, :], 2.0 * SLACK, None, ALU.add))
                    step(dve.tensor_tensor(least[:, 0, :], base0[0:1, :], least[:, 1, :], ALU.is_lt))
                    step(dve.tensor_tensor(least[:, 1, :], base0[0:1, :], least[:, 2, :], ALU.is_gt))
                    step(dve.tensor_tensor(least[:, 0, :], least[:, 0, :], least[:, 1, :], ALU.add))
                    step(dve.tensor_reduce(small[0:1, 3:4], least[:, 0, :], AX_X, ALU.add))
                    local = dst_local[:, :]
                    step(dve.tensor_tensor(local.rearrange("p (g c) -> p g c", c=GC),
                                           dst_f[:, 0:NG * GC].rearrange("p (g c) -> p g c", c=GC),
                                           base0[:, :].unsqueeze(2).to_broadcast([P, NG, GC]), ALU.subtract))
                    real = [(P, 0, EFULL)] + ([(EREM, EFULL, EFULL + 1)] if EREM else [])
                    for rows, c0, c1 in real:
                        if c1 > c0:
                            dve.tensor_scalar(outside[0:rows, 0, c0:c1], local[0:rows, c0:c1], 0.0, None, ALU.is_lt)
                            step(dve.tensor_scalar(outside[0:rows, 1, c0:c1], local[0:rows, c0:c1],
                                                   float(WINDOW - 1), None, ALU.is_gt))
                    step(dve.tensor_reduce(small[:, 0:1], outside[:, :, :].rearrange("p a c -> p (a c)"), AX_X, ALU.add))
                    from_first = outside[:, 0, 0:NDP]
                    step(dve.tensor_tensor(from_first, dst_f[:, C0:C0 + NDP], chunk_first[:], ALU.subtract))
                    step(dve.scalar_tensor_tensor(out=src_dst_key[:], in0=idx_f[:, 1, C0:C0 + NDP], scalar=float(CHUNK_W),
                                                  in1=from_first, op0=ALU.mult, op1=ALU.add))
                    step(dve.tensor_copy(src_lo[:], idx_f[:, 0, C0:C0 + NDP]))
                    for rows, c0, c1 in real:
                        if c1 > c0:
                            c0, c1 = max(c0, C0) - C0, c1 - C0
                            dve.tensor_scalar(chunk_out[0:rows, 0, c0:c1], from_first[0:rows, c0:c1], 0.0, None, ALU.is_lt)
                            step(dve.tensor_scalar(chunk_out[0:rows, 1, c0:c1], from_first[0:rows, c0:c1],
                                                   float(CHUNK_W - 1), None, ALU.is_gt))
                    step(dve.tensor_reduce(small[:, 4:5], chunk_out[:, :, :].rearrange("p a c -> p (a c)"), AX_X, ALU.add))
                    step(dve.tensor_tensor(small[:, 0:1], small[:, 0:1], small[:, 4:5], ALU.add))
                    step(dve.tensor_tensor(outside[0:1, 0, 0:NDP].rearrange("p (s c) -> p s c", c=SGC),
                                           chunk_first[0:1, :].rearrange("p (s c) -> p s c", c=SGC),
                                           base0[0:1, G0:NG:SG].unsqueeze(2).to_broadcast([1, NDP // SGC, SGC]),
                                           ALU.subtract))
                    step(dve.tensor_copy(chunk_at[:, :], outside[0:1, 0, 0:NDP]))
                    step(dve.tensor_scalar(chunk_row[:, 0, 0:ND], outside[0:1, 0, 0:ND], float(SGW - CHUNK_W), None,
                                           ALU.is_gt))
                    step(dve.tensor_tensor(chunk_row[:, 1, 1:ND], chunk_first[0:1, 1:ND], chunk_first[0:1, 0:ND - 1],
                                           ALU.is_le))
                    step(dve.tensor_reduce(small[0:1, 5:6], chunk_row[:, :, :].rearrange("p a c -> p (a c)"), AX_X, ALU.add))
                    step(dve.tensor_tensor(small[0:1, 0:1], small[0:1, 0:1], small[0:1, 5:6], ALU.add))
                    dve.tensor_tensor(small[0:1, 0:1], small[0:1, 0:1], small[0:1, 3:4], ALU.add).then_inc(s_viol, 1)

                def window_rounds():
                    dve.wait_ge(s_violT, 1)
                    step(dve.tensor_scalar(small[:, 1:2], bank[6][:, 510:511], 1.0, None, ALU.min))
                    dve.tensor_scalar(rounds_int[:, :], small[0:1, 1:2], float(ROUNDS - 1), 1.0, ALU.mult, ALU.add)
                    dve.tensor_scalar(base_step[:, :], small[:, 1:2], float(WINDOW), None, ALU.mult)
                    step(dve.tensor_scalar(small[:, 2:3], small[:, 1:2], -1.0, 1.0, ALU.mult, ALU.add))
                    step(dve.tensor_scalar(base0[:], base0[:], small[:, 2:3], None, ALU.mult))
                    dve.tensor_copy(base_int[:, :], base0[0:1, :])
                    step(dve.tensor_copy(base_cur[:], base0[:]))

                def logits():
                    dve.wait_ge(s_gate_in, 1)
                    step(dve.tensor_reduce(gate[:, 2, :], rel_rest[:, :, 0:D], AX_X, ALU.add))
                    dve.tensor_scalar(gate[:, 0, :], gate[:, 2, :], gate_bias[:, 0:1], None, ALU.add).then_inc(s_logit, 1)

                def gates():
                    dve.wait_ge(s_exp, 1)
                    step(dve.tensor_scalar(gate[:, 2, :], gate[:, 1, :], 1.0, None, ALU.add))
                    dve.reciprocal(gate[:, 3, :], gate[:, 2, :]).then_inc(s_gate, 1)

                dve.wait_ge(s_const, 6)
                step(dve.tensor_copy(iota_rep[:], iota_b[:, :].unsqueeze(2).to_broadcast([P, P, HC])))
                at_gate = min(n_hist - 1, 30)
                for i in range(n_hist):
                    c0, n = i * HC, min(HC, NCH - i * HC)
                    if i >= HBUF:
                        dve.wait_ge(s_hist, i - HBUF + 1)
                    dve.tensor_tensor(lo_hot[:, i % HBUF, :, 0:n], iota_rep[:, :, 0:n],
                                      idx_h[:, 0, c0:c0 + n].unsqueeze(1).to_broadcast([P, P, n]), ALU.is_equal)
                    dve.tensor_tensor(hi_hot[:, i % HBUF, :, 0:n], iota_rep[:, 0:NB, 0:n],
                                      idx_h[:, 1, c0:c0 + n].unsqueeze(1).to_broadcast([P, NB, n]),
                                      ALU.is_equal).then_inc(s_hot, 1)
                    if i == min(n_hist - 1, at_first + 4):
                        window_base()
                    if i == min(n_hist - 1, at_viol + 4):
                        window_rounds()
                    if i == max(0, at_gate - 2):
                        logits()
                    if i == at_gate:
                        gates()
                dve.wait_ge(s_hist, n_hist)
                dve.tensor_scalar(dsrc[:, 0, :], bank[7][:, 0:NB], 1.0, None, ALU.max).then_inc(s_deg1, 1)
                dve.wait_ge(s_sqrt, 1)
                step(dve.reciprocal(dsrc[:, 2, :], dsrc[:, 1, :]))
                dve.wait_ge(s_x, 16 * n_x_dmas)
                for i, (b0, n) in enumerate(batches):
                    dve.memset(x_rows[:, b0:b0 + n, D + 1:TW], 0.0)
                    for b in range(b0, b0 + n):
                        dve.tensor_scalar(x_rows[:, b, 0:D], x_rows[:, b, 0:D],
                                          dsrc[:, 2, b:b + 1], None, ALU.mult)
                    dve.tensor_copy(x_rows[:, b0:b0 + n, D], dsrc[:, 2, b0:b0 + n]).then_inc(s_scaled, 1)

            @block.tensor
            def _(pe):
                def turn_edges(a):
                    pe.wait_ge(s_rawf[a], 1)
                    for b in range(EB):
                        pe.transpose(bank[2 * a + b // 4][:, b % 4 * P:(b % 4 + 1) * P],
                                     rawf[:, a, b * P:(b + 1) * P], ident[:]).then_inc(s_edgeT[a], 1)

                pe.wait_ge(s_pool, 2)
                turn_edges(0)
                for i in range(n_hist):
                    pe.wait_ge(s_hot, i + 1)
                    for c in range(i * HC, min(NCH, (i + 1) * HC)):
                        rows = P if c < EFULL else EREM
                        last = pe.matmul(bank[7][:, 0:NB], lo_hot[0:rows, i % HBUF, :, c - i * HC],
                                         hi_hot[0:rows, i % HBUF, :, c - i * HC], start=(c == 0), stop=(c == NCH - 1))
                    last.then_inc(s_hist, 1)
                    if i == at_turn_edges:
                        turn_edges(1)
                        turn_edges(2)
                    if i == at_turn_w:
                        pe.wait_ge(s_w, 16 * n_w_dmas)
                        for j, n in enumerate(w_order):
                            if n in ("msg", "upd"):
                                pe.wait_ge(s_K, 1 if n == "msg" else 2)
                            if j:
                                pe.wait_ge(s_wT_cp, j)
                            for ih in range(DH):
                                for oh in range(DH):
                                    last = pe.transpose(turned_bank[:, ih * D + oh * P:ih * D + (oh + 1) * P],
                                                        w_raw[n][:, oh, ih * P:(ih + 1) * P], ident[:])
                            last.then_inc(s_wT, 1)
                    if i == at_first:
                        pe.wait_ge(s_dst_cp, 1)
                        pe.wait_ge(s_wT_cp, 6)
                        pe.matmul(bank[6][:, 0:NG], ones[0:1, :], dst_f[0:1, 0:NG * GC:GC],
                                  start=True, stop=True)
                        pe.matmul(bank[6][:, NG:NG + NDP], ones[0:1, :], dst_f[0:1, C0:C0 + NDP],
                                  start=True, stop=True).then_inc(s_first, 1)
                    if i == at_viol:
                        pe.wait_ge(s_viol, 2)
                        pe.wait_ge(s_first_cp, 1)
                        pe.matmul(bank[6][:, 510:511], ones[:, :], small[:, 0:1], start=True, stop=True).then_inc(s_violT, 1)
        setup.close()

        def end_of_stage(of_pool_dmas, sems):
            for s in of_pool_dmas:
                nc.gpsimd.dma_reset(range(s.num, s.num + 1))
            for s in sems:
                nc.gpsimd.sem_clear(s)
            nc.all_engine_barrier()

        def pass0_tiles():
            return (lent_rows("types_i", RP).bitcast(I32).rearrange("p (r e) -> p r e", r=TYPES),
                    lent_rows("types_h", RP).bitcast(F16).rearrange("p (r e) -> p r e", r=2),
                    lent_rows("type_hot", RP).bitcast(BF16).rearrange("p (r k e) -> p r k e", r=2, k=RK),
                    lent_rows("msg").rearrange("p (r c f) -> p r c f", r=2, c=GC))

        def edge_pass(k):
            first = k == 0
            ring = RING0 if first else RING
            table = table0 if first else tables[k - 1]
            width = TW if first else D
            with ExitStack() as tmp, ExitStack() as rctx:
                def lsem(name):
                    return rctx.enter_context(nc.semaphore(f"{name}_{k}"))

                rows = (lent_rows("rows").rearrange("p (r c f) -> p r c f", r=ring, c=GC) if first
                        else sb(f"rows{k}", [P, ring, GC, width], F32, tmp))
                hot = sb(f"hot{k}", [P, 2, GC, WINDOW], F32, tmp)
                s_rows = [lsem(f"s_rows{i}") for i in range(ring)]
                s_base = lsem("s_base")
                s_hot_d = lsem("s_hotd")
                s_seg = lsem("s_seg")
                s_add = lsem("s_add")
                s_free = lsem("s_free")
                pass_sems = s_rows + [s_base, s_hot_d, s_seg, s_add, s_free]
                if first:
                    types_i, types_h, type_hot, msg = pass0_tiles()
                    s_types = [lsem("s_types0"), lsem("s_types1")]
                    s_types_h = lsem("s_typesh")
                    s_type_hot = lsem("s_typehot")
                    s_rel_mm = lsem("s_relmm")
                    s_msg = lsem("s_msg")
                    s_init = lsem("s_init")
                    pass_sems += s_types + [s_types_h, s_type_hot, s_rel_mm, s_msg, s_init]
                else:
                    Wr, bl = ("W1r", "b1l") if k == 1 else ("W2r", "b2l")
                    HB = 3
                    h_in = sb(f"h_in{k}", [P, HB, D], F32, tmp)
                    hT = sb(f"hT{k}", [P, 2, DH, P], F32, tmp)
                    s_h = [lsem(f"s_h{i}") for i in range(HB)]
                    s_hT = lsem("s_hT")
                    s_hT_cp = lsem("s_hTcp")
                    s_z = lsem("s_z")
                    s_z_add = lsem("s_zadd")
                    pass_sems += s_h + [s_hT, s_hT_cp, s_z, s_z_add]
                    z_at = [[b for b in range(NB) if b * NG // NB == g] for g in range(NG)]

                def rows_full(g):
                    return 16 * sum(chunks_of(i) for i in range(g % ring, g + 1, ring))

                seg_bank = [bank[4], bank[5]]

                rounds = nc.values_load(rounds_int[0:1, 0:1], min_val=1, max_val=ROUNDS)
                with nc.Fori(0, rounds) as _round:
                    with nc.Block() as block:
                        @block.gpsimd
                        def _(pool):
                            for g in range(NG):
                                if g >= ring:
                                    pool.wait_ge(s_free, g - ring + 1)
                                for c in range(chunks_of(g)):
                                    col = g * GC + c
                                    pool.indirect_dma_start(
                                        out=rows[:, g % ring, c, :], out_offset=None, in_=table[:, :],
                                        in_offset=bass.IndirectOffsetOnAxis(ap=src_idx[:, col:col + 1], axis=0),
                                    ).then_inc(s_rows[g % ring], 16)

                        @block.sync
                        def _(sp):
                            if first:
                                sp.wait_ge(s_init, 1)
                                for g in range(NG):
                                    if g >= 2:
                                        sp.wait_ge(s_types_h, g - 1)
                                    n = min(GC * P, E - g * GC * P)
                                    sp.dma_start(types_i[:, g % TYPES, 0:n],
                                                 typ[g * GC * P:g * GC * P + n].rearrange("(a e) -> a e", a=1)
                                                 .to_broadcast([RP, n])).then_inc(s_types[g % 2], 16)
                            else:
                                for b in range(NB):
                                    if b >= HB:
                                        sp.wait_ge(s_hT, b - HB + 1)
                                    n = P if b < NFULL else NREM
                                    sp.dma_start(h_in[0:n, b % HB, :], table[b * P:b * P + n, :]
                                                 ).then_inc(s_h[b % HB], 16)

                        @block.scalar
                        def _(act):
                            if first:
                                for g in range(NG):
                                    act.wait_ge(s_types[g % 2], 16 * (g // 2 + 1))
                                    if g >= 2:
                                        act.wait_ge(s_type_hot, g - 1)
                                    act.copy(types_h[:, g % 2, :], types_i[:, g % TYPES, :]).then_inc(s_types_h, 1)
                            else:
                                for b in range(NB):
                                    act.wait_ge(s_hT, b + 1)
                                    if b >= 2:
                                        act.wait_ge(s_z, b - 1)
                                    act.copy(hT[:, b % 2, :, :].rearrange("p h n -> p (h n)"),
                                             bank[6][:, 0:D]).then_inc(s_hT_cp, 1)

                        @block.vector
                        def _(dve):
                            dve.tensor_tensor(dst_local[:, :].rearrange("p (g c) -> p g c", c=GC),
                                              dst_f[:, 0:NG * GC].rearrange("p (g c) -> p g c", c=GC),
                                              base_cur[:, :].unsqueeze(2).to_broadcast([P, NG, GC]),
                                              ALU.subtract).then_inc(s_base, 1)
                            dve.tensor_copy(base_int[:, :], base_cur[0:1, :]).then_inc(s_base, 1)
                            if first:
                                dve.memset(types_i, 0).then_inc(s_init, 1)
                                dve.memset(msg, 0.0).then_inc(s_base, 1)
                                dve.wait_ge(s_base, 3)
                                dve.memset(msg[:, :, :, D + SETW - 1], 1.0).then_inc(s_base, 1)
                            dve.wait_ge(s_base, 4 if first else 2)

                            def type_hots(g):
                                dve.wait_ge(s_types_h, g + 1)
                                if g >= 2:
                                    dve.wait_ge(s_rel_mm, GC * (g - 1))
                                for kk in range(RK):
                                    last = dve.tensor_scalar(type_hot[:, g % 2, kk, :], types_h[:, g % 2, :],
                                                             type_id[:, kk:kk + 1], None, ALU.is_equal)
                                last.then_inc(s_type_hot, 1)

                            def window_hots(g):
                                if g >= 2:
                                    dve.wait_ge(s_seg, g - 1)
                                dve.tensor_tensor(hot[:, g % 2, :, :],
                                                  iota_w[:, :].unsqueeze(1).to_broadcast([P, GC, WINDOW]),
                                                  dst_local[:, g * GC:(g + 1) * GC].unsqueeze(2)
                                                  .to_broadcast([P, GC, WINDOW]),
                                                  ALU.is_equal).then_inc(s_hot_d, 1)

                            def messages(g):
                                dve.wait_ge(s_rows[g % ring], rows_full(g))
                                if g >= 2:
                                    dve.wait_ge(s_seg, g - 1)
                                for c in range(chunks_of(g)):
                                    dve.wait_ge(s_rel_mm, GC * g + c + 1)
                                    last = dve.tensor_tensor(msg[:, g % 2, c, 0:D + 1], bank[c][:, 0:D + 1],
                                                             rows[:, g % ring, c, 0:D + 1], ALU.mult)
                                    last.then_inc(s_msg, 1)
                                dve.wait_ge(s_msg, GC * g + chunks_of(g))
                                dve.sem_inc(s_free, 1)

                            def add_window(g):
                                dve.wait_ge(s_seg, g + 1)
                                if g >= 1:
                                    dve.wait_ge(s_add, g)
                                at = dve.value_load(base_int[0:1, g:g + 1], min_val=0, max_val=N - 1)
                                ps = seg_bank[g % 2][:, 0:DH * WINDOW].rearrange("p (h w) -> p h w", h=DH)
                                if first:
                                    dst_row = seg_row[:, bass.ds(at, WINDOW)]
                                    dve.tensor_tensor(dst_row, dst_row,
                                                      seg_bank[g % 2][0:SETW, DH * WINDOW:(DH + 1) * WINDOW], ALU.add)
                                dst_cols = agg[:, :, bass.ds(at, WINDOW)]
                                dve.tensor_tensor(dst_cols, dst_cols, ps, ALU.add).then_inc(s_add, 1)

                            def z_add(b):
                                dve.wait_ge(s_z, b + 1)
                                dve.tensor_tensor(node_rows[:, b, :], bank[7][:, 0:D], bias[bl][:, :],
                                                  ALU.add).then_inc(s_z_add, 1)

                            if first:
                                type_hots(0)
                                for g in range(NG + 1):
                                    if g < NG:
                                        if g + 1 < NG:
                                            type_hots(g + 1)
                                        window_hots(g)
                                        messages(g)
                                    if g >= 1:
                                        add_window(g - 1)
                            else:
                                window_hots(0)
                                zb = 0
                                for g in range(NG):
                                    if g + 1 < NG:
                                        window_hots(g + 1)
                                    for b in z_at[g]:
                                        if b >= 1:
                                            z_add(b - 1)
                                    add_window(g)
                                z_add(NB - 1)
                            dve.wait_ge(s_add, NG)
                            dve.tensor_scalar(base_cur[:, :], base_cur[:, :], base_step[:, 0:1], None,
                                              ALU.add).then_inc(s_add, 1)
                            dve.wait_ge(s_add, NG + 1)

                        @block.tensor
                        def _(pe):
                            def relations(g):
                                pe.wait_ge(s_type_hot, g + 1)
                                for c in range(chunks_of(g)):
                                    if g >= 1:
                                        pe.wait_ge(s_msg, GC * (g - 1) + c + 1)
                                    for kk in range(RK):
                                        for part in range(3):
                                            last = pe.matmul(bank[c][:, 0:D + 1],
                                                             type_hot[:, g % 2, kk, c * P:(c + 1) * P],
                                                             rel_parts[:, kk, part, 0:D + 1],
                                                             start=(kk == 0 and part == 0),
                                                             stop=(kk == RK - 1 and part == 2))
                                    last.then_inc(s_rel_mm, 1)

                            def sums(g):
                                n = chunks_of(g)
                                pe.wait_ge(s_hot_d, g + 1)
                                if g >= 2:
                                    pe.wait_ge(s_add, g - 1)
                                if first:
                                    pe.wait_ge(s_msg, GC * g + n)
                                else:
                                    pe.wait_ge(s_rows[g % ring], rows_full(g))
                                data = msg[:, g % 2] if first else rows[:, g % ring]
                                for h in range(DH + first):
                                    lo, hi = (h * P, (h + 1) * P) if h < DH else (D, D + SETW)
                                    for c in range(n):
                                        last = pe.matmul(seg_bank[g % 2][0:hi - lo, h * WINDOW:(h + 1) * WINDOW],
                                                         data[:, c, lo:hi], hot[:, g % 2, c, :],
                                                         start=(c == 0), stop=(c == n - 1))
                                last.then_inc(s_seg, 1)
                                if not first:
                                    pe.wait_ge(s_seg, g + 1)
                                    pe.sem_inc(s_free, 1)

                            def z_turn(b):
                                n = P if b < NFULL else NREM
                                pe.wait_ge(s_h[b % HB], 16 * (b // HB + 1))
                                if b >= 1:
                                    pe.wait_ge(s_hT_cp, b)
                                for h in range(DH):
                                    last = pe.transpose(bank[6][:, h * P:h * P + n],
                                                        h_in[0:n, b % HB, h * P:(h + 1) * P], ident[0:n, 0:n])
                                last.then_inc(s_hT, 1)

                            def z_product(b):
                                pe.wait_ge(s_hT_cp, b + 1)
                                if b >= 1:
                                    pe.wait_ge(s_z_add, b)
                                for h in range(DH):
                                    last = pe.matmul(bank[7][:, 0:D], hT[:, b % 2, h, :], wT[Wr][:, h, :],
                                                     start=(h == 0), stop=(h == DH - 1))
                                last.then_inc(s_z, 1)

                            if first:
                                for g in range(NG + 1):
                                    if g < NG:
                                        relations(g)
                                    if g >= 1:
                                        sums(g - 1)
                            else:
                                for g in range(NG):
                                    for b in z_at[g]:
                                        z_turn(b)
                                        if b >= 1:
                                            z_product(b - 1)
                                    sums(g)
                                z_product(NB - 1)
                    end_of_stage(s_rows, pass_sems)

        BATCH = 4

        def node_stage(k):
            first, final = k == 0, k == 3
            Wl = ("msg", "W1l", "W2l", "W2l")[k]
            dest = out if final else tables[k]
            norm = first or final
            with ExitStack() as tmp:
                def lsem(name):
                    stage_sems.append(tmp.enter_context(nc.semaphore(f"{name}_n{k}")))
                    return stage_sems[-1]

                stage_sems = []

                vec = sb(f"vec{k}", [P, 2, D], F32, tmp)
                vT = sb(f"vT{k}", [P, 2, D], F32, tmp)
                stats = sb(f"stats{k}", [P, 2, 6], F32, tmp)
                mv = sb(f"mv{k}", [P, NB, 2], F32, tmp)
                std = sb(f"std{k}", [P, 3, NB], F32, tmp)
                degs = sb(f"degs{k}", [P, 3, NB], F32, tmp)
                RB = 4
                x1_in = sb(f"x1_in{k}", [P, RB, D], F32, tmp)
                s_pick, s_deg, s_dsq = lsem("s_pick"), lsem("s_deg"), lsem("s_dsq")
                s_a, s_a_free = lsem("s_a"), lsem("s_afree")
                s_vec, s_vT, s_vT_cp, s_o, s_y = (lsem(n) for n in ("s_vec", "s_vT", "s_vTcp", "s_o", "s_y"))
                s_c, s_var, s_std, s_ready = (lsem(n) for n in ("s_c", "s_var", "s_std", "s_ready"))
                s_store = lsem("s_store")
                s_clear = lsem("s_clear")
                s_x0 = lsem("s_x0")
                s_x1 = [lsem(f"s_x1{i}") for i in range(RB)] if final else []
                spans = [(b, min(BATCH, NB - b)) for b in range(0, NB, BATCH)]

                with nc.Block() as block:
                    @block.sync
                    def _(sp):
                        if first:
                            sp.wait_ge(s_x0, 16)
                            for b in range(0, NFULL, 8):
                                n = min(8, NFULL - b)
                                sp.dma_start(node_rows[:, b:b + n, :],
                                             x[b * P:(b + n) * P, :].rearrange("(b p) f -> p b f", p=P)).then_inc(s_x0, 16)
                            if NREM:
                                sp.dma_start(node_rows[0:NREM, NB - 1, :], x[NFULL * P:N, :]).then_inc(s_x0, 16)
                        if final:
                            for b in range(NB):
                                if b >= RB:
                                    sp.wait_ge(s_y, b - RB + 1)
                                n = P if b < NFULL else NREM
                                sp.dma_start(x1_in[0:n, b % RB, :], tables[0][b * P:b * P + n, :]
                                             ).then_inc(s_x1[b % RB], 16)

                    @block.scalar
                    def _(act):
                        if first:
                            act.wait_ge(s_deg, 1)
                            act.activation(degs[:, 1, :], degs[:, 0, :], ACT.Sqrt).then_inc(s_dsq, 1)
                        st = 0
                        span_of = {b0 + n - 1: i for i, (b0, n) in enumerate(spans)}

                        def finish(i):
                            b0, n = spans[i]
                            if norm:
                                act.wait_ge(s_var, i + 1)
                                act.activation(std[:, 1, b0:b0 + n], std[:, 0, b0:b0 + n],
                                               ACT.Sqrt).then_inc(s_std, 1)

                        for b in range(NB):
                            if first:
                                act.wait_ge(s_vT, b + 1)
                                if b >= 2:
                                    act.wait_ge(s_o, b - 1)
                                act.copy(vT[:, b % 2, :], bank[2 + b % 2][:, 0:D]).then_inc(s_vT_cp, 1)
                            if not norm:
                                act.wait_ge(s_y, b + 1)
                                act.activation(node_rows[:, b, :], node_rows[:, b, :], ACT.Relu).then_inc(s_ready, 1)
                            if b in span_of:
                                finish(span_of[b])

                    @block.gpsimd
                    def _(pool):
                        total = 0
                        for i, (b0, n) in enumerate(spans):
                            if not final:
                                pool.wait_ge(s_a, b0 + n)
                                pool.memset(agg[:, :, b0 * P:(b0 + n) * P], 0.0).then_inc(s_clear, 1)
                            pool.wait_ge(s_ready, b0 + n)
                            total += rows_out(pool, dest, node_rows[:, b0:b0 + n], b0, n, s_store)
                        pool.wait_ge(s_store, 16 * total)
                        if not final:
                            pool.wait_ge(s_clear, len(spans))

                    @block.vector
                    def _(dve):
                        done = [0]

                        def step(ins):
                            track(ins)
                            dve.wait_ge(s_c, done[0])

                        def track(ins):
                            done[0] += 1
                            ins.then_inc(s_c, 1)

                        if first:
                            dve.memset(node_rows[:, NB - 1, :], 0.0).then_inc(s_x0, 16)
                            dve.wait_ge(s_x0, 16 * (1 + n_x_dmas))
                            dve.wait_ge(s_pick, 1)
                            sd = bank[6][:, 0:2 * NB].rearrange("p (b t) -> p t b", t=2)
                            dve.tensor_copy(s_sum[:], sd[:, 0, :])
                            dve.tensor_scalar(degs[:, 0, :], sd[:, 1, :], 1.0, None, ALU.max).then_inc(s_deg, 1)
                            dve.wait_ge(s_deg, 1)
                            dve.reciprocal(rdeg[:], degs[:, 0, :])
                            dve.wait_ge(s_dsq, 1)
                            step(dve.reciprocal(ddst[:], degs[:, 1, :]))
                        step(dve.tensor_copy(base_cur[:], base0[:]))

                        def take(b):
                            dve.wait_ge(s_a, b + 1)
                            ps = bank[b % 2][:, 0:D]
                            if first:
                                if b >= 2:
                                    dve.wait_ge(s_vT, b - 1)
                                step(dve.scalar_tensor_tensor(out=vec[:, b % 2, :], in0=bias["msg"][:, :],
                                                              scalar=s_sum[:, b:b + 1], in1=ps,
                                                              op0=ALU.mult, op1=ALU.add))
                                dve.scalar_tensor_tensor(out=vec[:, b % 2, :], in0=vec[:, b % 2, :],
                                                         scalar=ddst[:, b:b + 1], in1=node_rows[:, b, :],
                                                         op0=ALU.mult, op1=ALU.add).then_inc(s_vec, 1)
                            else:
                                ins = dve.scalar_tensor_tensor(out=node_rows[:, b, :], in0=ps,
                                                               scalar=rdeg[:, b:b + 1], in1=node_rows[:, b, :],
                                                               op0=ALU.mult, op1=ALU.add)
                                if final:
                                    step(ins)
                                    dve.sem_inc(s_a_free, 1)
                                    dve.wait_ge(s_x1[b % RB], 16 * (b // RB + 1))
                                    n = P if b < NFULL else NREM
                                    step(dve.tensor_tensor(node_rows[0:n, b, :], node_rows[0:n, b, :],
                                                           x1_in[0:n, b % RB, :], ALU.add))
                                    dve.sem_inc(s_y, 1)
                                    moments(b)
                                else:
                                    ins.then_inc(s_y, 1)

                        def give(b):
                            dve.wait_ge(s_o, b + 1)
                            ps = bank[4 + b % 2][:, 0:D]
                            step(dve.tensor_tensor(node_rows[:, b, :], ps, node_rows[:, b, :], ALU.add))
                            dve.sem_inc(s_y, 1)
                            step(dve.tensor_tensor(node_rows[:, b, :], node_rows[:, b, :], bias["upd"][:, :], ALU.add))
                            moments(b)

                        def moments(b):
                            step(dve.bn_stats(stats[:, b % 2, :], node_rows[:, b, :]))
                            track(dve.bn_aggr(mv[:, b, :], stats[:, b % 2, :]))

                        def variance(i):
                            b0, n = spans[i]
                            dve.wait_ge(s_c, done[0])
                            step(dve.tensor_scalar(std[:, 0, b0:b0 + n], mv[:, b0:b0 + n, 1], LN_EPS, None, ALU.add))
                            dve.sem_inc(s_var, 1)

                        def normalise(i):
                            b0, n = spans[i]
                            dve.wait_ge(s_std, i + 1)
                            step(dve.reciprocal(std[:, 2, b0:b0 + n], std[:, 1, b0:b0 + n]))
                            for b in range(b0, b0 + n):
                                dve.tensor_scalar(node_rows[:, b, :], node_rows[:, b, :], mv[:, b, 0:1],
                                                  std[:, 2, b:b + 1], ALU.subtract, ALU.mult).then_inc(s_ready, 1)

                        if first:
                            pending = []
                            for b in range(NB + 2):
                                if b < NB:
                                    take(b)
                                if b >= 2:
                                    c = b - 2
                                    give(c)
                                    if pending:
                                        normalise(pending.pop())
                                    if c % BATCH == BATCH - 1 or c == NB - 1:
                                        variance(c // BATCH)
                                        pending.append(c // BATCH)
                            normalise(pending.pop())
                        elif final:
                            pending = []
                            for b in range(NB):
                                take(b)
                                if pending:
                                    normalise(pending.pop())
                                if b % BATCH == BATCH - 1 or b == NB - 1:
                                    variance(b // BATCH)
                                    pending.append(b // BATCH)
                            normalise(pending.pop())
                        else:
                            for b in range(NB):
                                take(b)

                    @block.tensor
                    def _(pe):
                        if first:
                            for b in range(NB):
                                last = pe.matmul(bank[6][:, 2 * b:2 * b + 2], seg_row[:, b * P:(b + 1) * P],
                                                 pick[:, :], start=True, stop=True)
                            last.then_inc(s_pick, 1)

                        def product(b):
                            if b >= 2:
                                pe.wait_ge(s_vec if first else (s_a_free if final else s_y), b - 1)
                            for h in range(DH):
                                last = pe.matmul(bank[b % 2][:, 0:D], agg[:, h, b * P:(b + 1) * P], wT[Wl][:, h, :],
                                                 start=(h == 0), stop=(h == DH - 1))
                            last.then_inc(s_a, 1)

                        def turn(b):
                            pe.wait_ge(s_vec, b + 1)
                            if b >= 2:
                                pe.wait_ge(s_vT_cp, b - 1)
                            for h in range(DH):
                                last = pe.transpose(bank[2 + b % 2][:, h * P:(h + 1) * P],
                                                    vec[:, b % 2, h * P:(h + 1) * P], ident[:])
                            last.then_inc(s_vT, 1)

                        def update(b):
                            pe.wait_ge(s_vT_cp, b + 1)
                            if b >= 2:
                                pe.wait_ge(s_y, b - 1)
                            for h in range(DH):
                                last = pe.matmul(bank[4 + b % 2][:, 0:D], vT[:, b % 2, h * P:(h + 1) * P],
                                                 wT["upd"][:, h, :], start=(h == 0), stop=(h == DH - 1))
                            last.then_inc(s_o, 1)

                        if first:
                            for b in range(NB + 2):
                                if b < NB:
                                    product(b)
                                if 1 <= b <= NB:
                                    turn(b - 1)
                                if b >= 2:
                                    update(b - 2)
                        else:
                            for b in range(NB):
                                product(b)
                end_of_stage([s_store], stage_sems)

        def one_round_layer(k):
            first, final = k == 0, k == 3
            norm = first or final
            ring = RING0 if first else RING
            table = table0 if first else tables[k - 1]
            dest = out if final else tables[k]
            width = TW if first else D
            Wl = ("msg", "W1l", "W2l", "W2l")[k]
            WORK = 4 if first else 5
            groups = NG if first else G0
            units = 0 if first else WD * NB
            unit_slot = [3 + u * (groups - 3 - EARLY) // units for u in range(units)]
            added_slot = [unit_slot[NB * (w + 1) - 1] for w in range(0 if first else WD)]
            last_group, last_dense = [], []
            for b in range(NB):
                last_group.append(max([g for g in range(groups) if first_dst_at_least(g) < P * (b + 1)
                                       and (first or dst_below(g) > P * b)], default=-1))
                last_dense.append(max([w for w in range(len(added_slot)) if
                                       first_dst_at_least(G0 + SG * DW * w) < P * (b + 1)], default=-1))
            ready = [max(last_group[b] + 2, added_slot[last_dense[b]] + 1 if last_dense[b] >= 0 else 0) for b in range(NB)]
            order = sorted(range(NB), key=lambda b: (ready[b], b))
            start = []
            for j, b in enumerate(order):
                start.append(max([ready[b]] + ([start[j - 1] + 1 + first] if j else []) +
                                 ([start[j - WORK] + 10] if j >= WORK and norm else [])))
            slots = max(start[-1] + 8, groups + 2)

            def at(slot, after):
                return [j for j in range(NB) if start[j] + after == slot]

            def rows_of(j):
                return P if order[j] < NFULL else NREM

            def counts_at(slot):
                return [i for i in range(ND if first else 0) if i * NG // ND == slot]

            halves = ((0, HH), (HH, NB))

            split_step = [unit_slot[i * HBATCH] for i in range(ceil_div(NB, HBATCH))] if not first else []
            split_slot = [max(0, i * min(3, (t - 3) // max(i, 1))) for i, t in enumerate(split_step)]
            assert all(a + 2 < t for a, t in zip(split_slot, split_step))
            batches_h = [(b, min(HBATCH, NB - b)) for b in range(0, NB, HBATCH)]

            def pool_rel(g):
                return [c for c in POOL_REL[g % len(POOL_REL)] if c < chunks_of(g)] if first else []

            made = [(g, c) for g in range(NG) for c in range(chunks_of(g)) if c not in pool_rel(g)] if first else []

            def products(g):
                return sum(chunks_of(i) - len(pool_rel(i)) for i in range(g))

            with ExitStack() as tmp:
                layer_sems = []

                def lsem(name):
                    layer_sems.append(tmp.enter_context(nc.semaphore(f"{name}_f{k}")))
                    return layer_sems[-1]

                hot = sb(f"fhot{k}", [P, 2, GC, WINDOW], F32, tmp)
                stats = sb(f"fstats{k}", [P, 2, 6], F32, tmp)
                mv = sb(f"fmv{k}", [P, NB, 2], F32, tmp)
                rstd = sb(f"frstd{k}", [P, 2, NB], F32, tmp)
                work = sb(f"work{k}", [P, WORK, D], F32, tmp)
                s_rows = [lsem(f"s_rows{i}") for i in range(ring)]
                s_start, s_hot_d, s_seg, s_add, s_free = (lsem(n) for n in ("s_start", "s_hotd", "s_seg", "s_add", "s_free"))
                s_c, s_a, s_take, s_y, s_var, s_std, s_ready = (
                    lsem(n) for n in ("s_c", "s_a", "s_take", "s_y", "s_var", "s_std", "s_ready"))
                s_work = [lsem(f"s_work{i}") for i in range(WORK)] if norm else []
                s_store = [lsem(f"s_store{i}") for i in range(WORK)]
                if first:
                    rows = lent_rows("rows").rearrange("p (r c f) -> p r c f", r=ring, c=GC)
                    rel_rows = lent_rows("rel_rows").rearrange("p (r c f) -> p r c f", r=ring, c=max(map(len, POOL_REL)))
                    types_i, types_h, type_hot, msg = pass0_tiles()
                    vec = sb("fvec", [P, 2, D], F32, tmp)
                    vT = sb("fvT", [P, 2, D], F32, tmp)
                    degs = sb("fdegs", [P, NB], F32, tmp)
                    s_types = [lsem(f"s_types{i}") for i in range(TYPES)]
                    s_types_h, s_type_hot, s_rel_mm, s_msg = (lsem(n) for n in ("s_typesh", "s_typehot", "s_relmm", "s_msg"))
                    lo_hot = sb("flo_hot", [P, 2, P], BF16, tmp)
                    key_hot = sb("fkey_hot", [P, 2, NB * CHUNK_W], BF16, tmp)
                    count = sb("fcount", [P, COUNT_BUFS, HH, SGW], BF16, tmp)
                    s_count_hot, s_count, s_counted = (lsem(n) for n in ("s_count_hot", "s_count", "s_counted"))
                    s_count_out = [lsem(f"s_count_out{i}") for i in range(COUNT_BUFS)]
                    s_rdeg, s_ddst, s_vT, s_vT_cp, s_o = (
                        lsem(n) for n in ("s_rdeg", "s_ddst", "s_vT", "s_vTcp", "s_o"))
                else:
                    rows = sb(f"frows{k}", [P, ring, GC, width], F32, tmp)
                    Wr, bl = ("W1r", "b1l") if k == 1 else ("W2r", "b2l")
                    HB = 2
                    h_in = sb(f"fh_in{k}", [P, HB, D], F32, tmp)
                    hT = sb(f"fhT{k}", [P, 2, D], F32, tmp)
                    parts = (lent_rows("parts", P, split_w).bitcast(BF16)
                             .rearrange("p (b a f) -> p b a f", b=NB, a=3))
                    h_batch = lent_rows("h_batch", P, split_w).rearrange("p (r b f) -> p r b f", r=2, b=HBATCH)
                    count_tile = sb(f"fcounts{k}", [P, ATILES, DW, HTILE, SGW], BF16, tmp)
                    s_h = [lsem(f"s_h{i}") for i in range(HB)]
                    s_batch = [lsem(f"s_batch{i}") for i in range(2)]
                    s_tile = [lsem(f"s_tile{i}") for i in range(ATILES)]
                    s_hT, s_hT_cp, s_z = (lsem(n) for n in ("s_hT", "s_hTcp", "s_z"))
                    s_part1, s_rest, s_part2, s_parts, s_tile_used, s_dense_added = (
                        lsem(n) for n in ("s_part1", "s_rest", "s_part2", "s_parts", "s_tile_used", "s_dense_added"))
                seg_bank = [bank[4], bank[5]]
                sum_bank = [bank[6], bank[6]] if first else [bank[0], bank[1]]

                def rows_full(g):
                    return 16 * sum(chunks_of(i) + len(pool_rel(i)) for i in range(g % ring, g + 1, ring))

                def node_tile(j):
                    return work[:, j % WORK, :]

                def tile_of(u):
                    return u // NB * TPW + u % NB // HTILE

                def batch_dmas(i):
                    b, n = batches_h[i]
                    return out_dmas(b, n)

                with nc.Block() as block:
                    @block.gpsimd
                    def _(pool):
                        for g in range(groups):
                            if g >= ring:
                                pool.wait_ge(s_free, g - ring + 1)
                            for c in range(chunks_of(g)):
                                col = g * GC + c
                                pool.indirect_dma_start(
                                    out=rows[:, g % ring, c, :], out_offset=None, in_=table[:, :],
                                    in_offset=bass.IndirectOffsetOnAxis(ap=src_idx[:, col:col + 1], axis=0),
                                ).then_inc(s_rows[g % ring], 16)
                            for i, c in enumerate(pool_rel(g)):
                                col = g * GC + c
                                pool.indirect_dma_start(
                                    out=rel_rows[:, g % ring, i, :], out_offset=None, in_=table_rel[:, :],
                                    in_offset=bass.IndirectOffsetOnAxis(ap=type_idx[:, col:col + 1], axis=0),
                                ).then_inc(s_rows[g % ring], 16)

                    @block.sync
                    def _(sp):
                        def load_types(g):
                            if g >= TYPES:
                                sp.wait_ge(s_types_h, g - TYPES + 1)
                            n = min(GC * P, E - g * GC * P)
                            sp.dma_start(types_i[:, g % TYPES, 0:n],
                                         typ[g * GC * P:g * GC * P + n].rearrange("(a e) -> a e", a=1)
                                         .to_broadcast([RP, n])).then_inc(s_types[g % TYPES], 16)

                        def load_h(j):
                            if j >= HB:
                                sp.wait_ge(s_hT, j - HB + 1)
                            n, b = rows_of(j), order[j]
                            sp.dma_start(h_in[0:n, j % HB, :], table[b * P:b * P + n, :]).then_inc(s_h[j % HB], 16)

                        def load_work(j):
                            if j >= WORK:
                                sp.wait_ge(s_store[j % WORK], 16 * (j // WORK))
                            n, b = rows_of(j), order[j]
                            of = x if first else tables[0]
                            sp.dma_start(work[0:n, j % WORK, :], of[b * P:b * P + n, :]).then_inc(s_work[j % WORK], 16)

                        def store(j):
                            sp.wait_ge(s_ready, j + 1)
                            n, b = rows_of(j), order[j]
                            sp.dma_start(dest[b * P:b * P + n, :], node_tile(j)[0:n, :]).then_inc(s_store[j % WORK], 16)

                        def load_batch(i):
                            if i >= 2:
                                sp.wait_ge(s_parts, i - 1)
                            b, n = batches_h[i]
                            full = max(0, min(n, NFULL - b))
                            if full:
                                sp.dma_start(h_batch[:, i % 2, 0:full, :],
                                             table[b * P:(b + full) * P, :].rearrange("(b p) f -> p b f", p=P)
                                             ).then_inc(s_batch[i % 2], 16)
                            if full < n:
                                sp.dma_start(h_batch[0:NREM, i % 2, full, :],
                                             table[NFULL * P:N, :]).then_inc(s_batch[i % 2], 16)

                        def load_tile(t):
                            if t >= ATILES:
                                sp.wait_ge(s_tile_used, t - ATILES + 1)
                            w, hi = t // TPW, t % TPW * HTILE
                            n = min(HTILE, NB - hi)
                            sp.dma_start(count_tile[:, t % ATILES, :, 0:n, :],
                                         counts[w * DW:(w + 1) * DW, :, hi:hi + n, :].rearrange("s p h c -> p s h c")
                                         ).then_inc(s_tile[t % ATILES], 16)

                        def store_counts(sg):
                            sp.wait_ge(s_counted, min(ND, (sg + 1) * SGC))
                            for h, (lo, hi) in enumerate(halves):
                                buf = (2 * sg + h) % COUNT_BUFS
                                sp.dma_start(counts[sg, :, lo:hi, :], count[:, buf, 0:hi - lo, :]
                                             ).then_inc(s_count_out[buf], 16)

                        sp.wait_ge(s_start, 1)
                        for g in range(min(TYPES + 1, NG) if first else 0):
                            load_types(g)
                        for s in range(slots):
                            if first and s + TYPES + 1 < NG:
                                load_types(s + TYPES + 1)
                            if first:
                                for i in counts_at(s):
                                    if i == ND - 1 or (i + 1) % SGC == 0:
                                        store_counts(i // SGC)
                            else:
                                for i in range(len(batches_h)):
                                    if s == (split_slot[i - 1] if i else 0):
                                        load_batch(i)
                                if s == 0:
                                    for t in range(ATILES):
                                        load_tile(t)
                                for t in range(ATILES, WD * TPW):
                                    last_unit = max(u for u in range(units) if tile_of(u) == t - ATILES)
                                    if unit_slot[last_unit] == s:
                                        load_tile(t)
                                for j in range(NB):
                                    if max(0, start[j] - 3) == s:
                                        load_h(j)
                            if norm:
                                for j in range(NB):
                                    if max(0, start[j] - 2) == s:
                                        load_work(j)
                            for j in at(s, 7 if norm else 2):
                                store(j)
                        for i in range(min(WORK, NB)):
                            sp.wait_ge(s_store[i], 16 * len(range(i, NB, WORK)))
                        for i in range(COUNT_BUFS if first else 0):
                            sp.wait_ge(s_count_out[i], 16 * len(range(i, 2 * WD * DW, COUNT_BUFS)))

                    @block.scalar
                    def _(act):
                        for s in range(slots):
                            if first and s < NG:
                                for g in ([0, 1, 2] if s == 0 else [s + 2]):
                                    if g < NG:
                                        act.wait_ge(s_types[g % TYPES], 16 * (g // TYPES + 1))
                                        if g >= 2:
                                            act.wait_ge(s_type_hot, g - 1)
                                        act.copy(types_h[:, g % 2, :], types_i[:, g % TYPES, :]).then_inc(s_types_h, 1)
                            if not first:
                                for i, (b, n) in enumerate(batches_h):
                                    half = h_batch[:, i % 2, 0:n, :]
                                    if s == split_slot[i]:
                                        act.wait_ge(s_batch[i % 2], 16 * sum(batch_dmas(q) for q in range(i % 2, i + 1, 2)))
                                        act.copy(parts[:, b:b + n, 0, :], half).then_inc(s_part1, 1)
                                    if s == split_slot[i] + 1:
                                        act.wait_ge(s_rest, i + 1)
                                        act.copy(parts[:, b:b + n, 1, :], half).then_inc(s_part2, 1)
                                for j in at(s, -1):
                                    act.wait_ge(s_hT, j + 1)
                                    if j >= 2:
                                        act.wait_ge(s_z, j - 1)
                                    act.copy(hT[:, j % 2, :], bank[6][:, 0:D]).then_inc(s_hT_cp, 1)
                            if first:
                                for b in at(s, 1):
                                    act.wait_ge(s_rdeg, b + 1)
                                    act.activation(ddst[:, b:b + 1], rdeg[:, b:b + 1], ACT.Sqrt).then_inc(s_ddst, 1)
                                for b in at(s, 3):
                                    act.wait_ge(s_vT, b + 1)
                                    if b >= 2:
                                        act.wait_ge(s_o, b - 1)
                                    act.copy(vT[:, b % 2, :], bank[7][:, 0:D]).then_inc(s_vT_cp, 1)
                            if norm:
                                for b in at(s, 5):
                                    act.wait_ge(s_var, b + 1)
                                    act.activation(rstd[:, 1, b:b + 1], rstd[:, 0, b:b + 1], ACT.Sqrt).then_inc(s_std, 1)
                            else:
                                for b in at(s, 1):
                                    act.wait_ge(s_y, b + 1)
                                    act.activation(node_tile(b), node_tile(b), ACT.Relu).then_inc(s_ready, 1)

                    @block.vector
                    def _(dve):
                        done = [0]

                        def track(ins):
                            done[0] += 1
                            ins.then_inc(s_c, 1)

                        def step(ins):
                            track(ins)
                            dve.wait_ge(s_c, done[0])

                        if first:
                            dve.memset(types_i, 0)
                            step(dve.memset(msg, 0.0))
                            step(dve.memset(msg[:, :, :, D + SETW - 1], 1.0))
                            dve.memset(work[:], 0.0).then_inc(s_start, 1)
                        else:
                            step(dve.memset(h_in[:], 0.0))
                            step(dve.memset(h_batch, 0.0))
                            dve.memset(work[:], 0.0).then_inc(s_start, 1)

                        def type_hots(g):
                            lo, hi = len(pool_rel(g)) * P, chunks_of(g) * P
                            dve.wait_ge(s_types_h, g + 1)
                            if g >= 2:
                                dve.wait_ge(s_rel_mm, products(g - 1))
                            if lo == hi:
                                dve.sem_inc(s_type_hot, 1)
                                return
                            for kk in range(RK):
                                last = dve.tensor_scalar(type_hot[:, g % 2, kk, lo:hi], types_h[:, g % 2, lo:hi],
                                                         type_id[:, kk:kk + 1], None, ALU.is_equal)
                            last.then_inc(s_type_hot, 1)

                        def window_hots(g):
                            if g >= 2:
                                dve.wait_ge(s_seg, g - 1)
                            dve.tensor_tensor(hot[:, g % 2, :, :],
                                              iota_w[:, :].unsqueeze(1).to_broadcast([P, GC, WINDOW]),
                                              dst_local[:, g * GC:(g + 1) * GC].unsqueeze(2)
                                              .to_broadcast([P, GC, WINDOW]),
                                              ALU.is_equal).then_inc(s_hot_d, 1)

                        def messages(g):
                            dve.wait_ge(s_rows[g % ring], rows_full(g))
                            if g >= 2:
                                dve.wait_ge(s_seg, g - 1)
                            for c in range(chunks_of(g)):
                                if c in pool_rel(g):
                                    relation = rel_rows[:, g % ring, pool_rel(g).index(c), 0:D + 1]
                                else:
                                    r = products(g) + c - len(pool_rel(g))
                                    dve.wait_ge(s_rel_mm, r + 1)
                                    relation = bank[r % 2][:, 0:D + 1]
                                dve.tensor_tensor(msg[:, g % 2, c, 0:D + 1], relation,
                                                  rows[:, g % ring, c, 0:D + 1], ALU.mult).then_inc(s_msg, 1)
                            dve.wait_ge(s_msg, GC * g + chunks_of(g))
                            dve.sem_inc(s_free, 1)

                        def add_window(g):
                            at_col = dve.value_load(base_int[0:1, g:g + 1], min_val=0, max_val=N - 1)
                            dve.wait_ge(s_seg, g + 1)
                            if g >= 1:
                                dve.wait_ge(s_add, g)
                            ps = seg_bank[g % 2][:, 0:DH * WINDOW].rearrange("p (h w) -> p h w", h=DH)
                            if first:
                                dst_row = seg_row[:, bass.ds(at_col, WINDOW)]
                                dve.tensor_tensor(dst_row, dst_row,
                                                  seg_bank[g % 2][0:SETW, DH * WINDOW:(DH + 1) * WINDOW], ALU.add)
                            dst_cols = agg[:, :, bass.ds(at_col, WINDOW)]
                            dve.tensor_tensor(dst_cols, dst_cols, ps, ALU.add).then_inc(s_add, 1)

                        def count_hots(i):
                            if i >= 2:
                                dve.wait_ge(s_count, i - 1)
                            dve.tensor_scalar(lo_hot[:, i % 2, :], iota_b[:, :], src_lo[:, i:i + 1], None, ALU.is_equal)
                            dve.tensor_scalar(key_hot[:, i % 2, :], iota_key[:, :], src_dst_key[:, i:i + 1], None,
                                              ALU.is_equal).then_inc(s_count_hot, 1)

                        def count_add(i):
                            sg = i // SGC
                            if i % SGC == 0:
                                for h in range(2):
                                    q = 2 * sg + h
                                    if q >= COUNT_BUFS:
                                        dve.wait_ge(s_count_out[q % COUNT_BUFS], 16 * (q // COUNT_BUFS))
                                    step(dve.memset(count[:, q % COUNT_BUFS], 0.0))
                            at_col = dve.value_load(chunk_at[0:1, i:i + 1], min_val=0, max_val=SGW - CHUNK_W)
                            dve.wait_ge(s_count, i + 1)
                            if i:
                                dve.wait_ge(s_counted, i)
                            for h, (lo, hi) in enumerate(halves):
                                cols = count[:, (2 * sg + h) % COUNT_BUFS, 0:hi - lo, bass.ds(at_col, CHUNK_W)]
                                last = dve.tensor_tensor(cols, cols, bank[2 + h][:, 0:(hi - lo) * CHUNK_W]
                                                         .rearrange("p (s w) -> p s w", w=CHUNK_W), ALU.add)
                            last.then_inc(s_counted, 1)

                        def split_rest(i):
                            b, n = batches_h[i]
                            half = h_batch[:, i % 2, 0:n, :]
                            dve.wait_ge(s_part1, i + 1)
                            dve.tensor_tensor(half, half, parts[:, b:b + n, 0, :], ALU.subtract).then_inc(s_rest, 1)

                        def split_last(i):
                            b, n = batches_h[i]
                            dve.wait_ge(s_part2, i + 1)
                            dve.wait_ge(s_rest, i + 1)
                            dve.tensor_tensor(parts[:, b:b + n, 2, :], h_batch[:, i % 2, 0:n, :],
                                              parts[:, b:b + n, 1, :], ALU.subtract).then_inc(s_parts, 1)

                        def add_dense(w):
                            dve.wait_ge(s_tile_used, (w + 1) * TPW)
                            dve.wait_ge(s_add, min(s_now[0], groups))
                            for q in range(DW):
                                g = G0 + SG * (DW * w + q)
                                at_col = dve.value_load(base_int[0:1, g:g + 1], min_val=0, max_val=N - 1)
                                for h in range(DH):
                                    cols = agg[:, h, bass.ds(at_col, SGW)]
                                    last = dve.tensor_tensor(cols, cols, bank[2 + h][:, q * SGW:(q + 1) * SGW], ALU.add)
                                    track(last)
                                dve.wait_ge(s_c, done[0])
                            dve.sem_inc(s_dense_added, 1)

                        def degrees(b):
                            dve.wait_ge(s_a, b + 1)
                            dve.tensor_copy(s_sum[:, b:b + 1], bank[6][:, D:D + 1])
                            step(dve.tensor_scalar(degs[:, b:b + 1], bank[6][:, D + 1:D + 2], 1.0, None, ALU.max))
                            dve.reciprocal(rdeg[:, b:b + 1], degs[:, b:b + 1]).then_inc(s_rdeg, 1)

                        def clear(b):
                            dve.memset(agg[:, :, b * P:(b + 1) * P], 0.0)

                        def take(b):
                            dve.wait_ge(s_a, b + 1)
                            ps = sum_bank[b % 2][:, 0:D]
                            if first:
                                dve.wait_ge(s_ddst, b + 1)
                                dve.wait_ge(s_work[b % WORK], 16 * (b // WORK + 1))
                                if b >= 2:
                                    dve.wait_ge(s_vT, b - 1)
                                step(dve.scalar_tensor_tensor(out=vec[:, b % 2, :], in0=bias["msg"][:, :],
                                                              scalar=s_sum[:, b:b + 1], in1=ps,
                                                              op0=ALU.mult, op1=ALU.add))
                                dve.scalar_tensor_tensor(out=vec[:, b % 2, :], in0=vec[:, b % 2, :],
                                                         scalar=ddst[:, b:b + 1], in1=node_tile(b),
                                                         op0=ALU.mult, op1=ALU.add).then_inc(s_take, 1)
                            else:
                                dve.wait_ge(s_z, b + 1)
                                other = bias[bl][:, :]
                                if final:
                                    dve.wait_ge(s_work[b % WORK], 16 * (b // WORK + 1))
                                    other = node_tile(b)
                                elif b >= WORK:
                                    dve.wait_ge(s_store[b % WORK], 16 * (b // WORK))
                                step(dve.scalar_tensor_tensor(out=node_tile(b), in0=ps,
                                                              scalar=rdeg[:, order[b]:order[b] + 1], in1=other,
                                                              op0=ALU.mult, op1=ALU.add))
                                step(dve.tensor_tensor(node_tile(b), node_tile(b), bank[7][:, 0:D], ALU.add))
                                dve.sem_inc(s_take, 1)
                                if final:
                                    step(dve.tensor_tensor(node_tile(b), node_tile(b), bias[bl][:, :], ALU.add))
                                dve.sem_inc(s_y, 1)
                            if not final:
                                clear(order[b])

                        def give(b):
                            dve.wait_ge(s_o, b + 1)
                            y = node_tile(b)
                            step(dve.tensor_tensor(y, bank[7][:, 0:D], y, ALU.add))
                            dve.sem_inc(s_y, 1)
                            step(dve.tensor_tensor(y, y, bias["upd"][:, :], ALU.add))

                        def moments(b):
                            step(dve.bn_stats(stats[:, b % 2, :], node_tile(b)))
                            step(dve.bn_aggr(mv[:, b, :], stats[:, b % 2, :]))
                            step(dve.tensor_scalar(mv[:, b, 1:2], mv[:, b, 1:2], LN_EPS, None, ALU.add))
                            dve.reciprocal(rstd[:, 0, b:b + 1], mv[:, b, 1:2]).then_inc(s_var, 1)

                        def normalise(b):
                            dve.wait_ge(s_std, b + 1)
                            dve.tensor_scalar(node_tile(b), node_tile(b), mv[:, b, 0:1], rstd[:, 1, b:b + 1],
                                              ALU.subtract, ALU.mult).then_inc(s_ready, 1)

                        if first:
                            for g in range(min(2, NG)):
                                type_hots(g)
                            for i in counts_at(0):
                                count_hots(i)
                        else:
                            window_hots(0)
                        s_now = [0]
                        for s in range(slots):
                            s_now[0] = s + 1
                            if first:
                                if s < NG:
                                    messages(s)
                                if s + 2 < NG:
                                    type_hots(s + 2)
                                if s < NG:
                                    window_hots(s)
                                for i in counts_at(s):
                                    count_add(i)
                                for i in counts_at(s + 1):
                                    count_hots(i)
                                if 1 <= s <= NG:
                                    add_window(s - 1)
                            else:
                                if s + 1 < groups:
                                    window_hots(s + 1)
                                for i in range(len(batches_h)):
                                    if split_slot[i] + 1 == s:
                                        split_rest(i)
                                    if split_slot[i] + 2 == s:
                                        split_last(i)
                                if s < groups:
                                    add_window(s)
                                if s in added_slot:
                                    add_dense(added_slot.index(s))
                            if first:
                                for b in at(s, 2):
                                    take(b)
                                for b in at(s, 1):
                                    degrees(b)
                                for b in at(s, 5):
                                    give(b)
                                    moments(b)
                            else:
                                for b in at(s, 1):
                                    take(b)
                                    if final:
                                        moments(b)
                            if norm:
                                for b in at(s, 6):
                                    normalise(b)
                        dve.wait_ge(s_c, done[0])

                    @block.tensor
                    def _(pe):
                        def relations(g):
                            pe.wait_ge(s_type_hot, g + 1)
                            for c in range(chunks_of(g)):
                                if c in pool_rel(g):
                                    continue
                                r = products(g) + c - len(pool_rel(g))
                                if r >= 2:
                                    before, chunk = made[r - 2]
                                    pe.wait_ge(s_msg, GC * before + chunk + 1)
                                for kk in range(RK):
                                    for part in range(3):
                                        last = pe.matmul(bank[r % 2][:, 0:D + 1],
                                                         type_hot[:, g % 2, kk, c * P:(c + 1) * P],
                                                         rel_parts[:, kk, part, 0:D + 1],
                                                         start=(kk == 0 and part == 0),
                                                         stop=(kk == RK - 1 and part == 2))
                                last.then_inc(s_rel_mm, 1)

                        def sums(g):
                            n = chunks_of(g)
                            pe.wait_ge(s_hot_d, g + 1)
                            if g >= 2:
                                pe.wait_ge(s_add, g - 1)
                            if first:
                                pe.wait_ge(s_msg, GC * g + n)
                            else:
                                pe.wait_ge(s_rows[g % ring], rows_full(g))
                            data = msg[:, g % 2] if first else rows[:, g % ring]
                            for h in range(DH + first):
                                lo, hi = (h * P, (h + 1) * P) if h < DH else (D, D + SETW)
                                for c in range(n):
                                    last = pe.matmul(seg_bank[g % 2][0:hi - lo, h * WINDOW:(h + 1) * WINDOW],
                                                     data[:, c, lo:hi], hot[:, g % 2, c, :],
                                                     start=(c == 0), stop=(c == n - 1))
                            last.then_inc(s_seg, 1)

                        def free(g):
                            pe.wait_ge(s_seg, g + 1)
                            pe.sem_inc(s_free, 1)

                        def count_product(i):
                            pe.wait_ge(s_count_hot, i + 1)
                            if i:
                                pe.wait_ge(s_counted, i)
                            for h, (lo, hi) in enumerate(halves):
                                last = pe.matmul(bank[2 + h][:, 0:(hi - lo) * CHUNK_W], lo_hot[:, i % 2, :],
                                                 key_hot[:, i % 2, lo * CHUNK_W:hi * CHUNK_W], start=True, stop=True)
                            last.then_inc(s_count, 1)

                        def dense_unit(u):
                            w, b, t = u // NB, u % NB, tile_of(u)
                            if w == 0 and b % HBATCH == 0:
                                pe.wait_ge(s_parts, b // HBATCH + 1)
                            if b % HTILE == 0:
                                pe.wait_ge(s_tile[t % ATILES], 16 * (t // ATILES + 1))
                            if b == 0 and w:
                                pe.wait_ge(s_dense_added, w)
                            for h in range(DH):
                                for part in range(3):
                                    last = pe.matmul(bank[2 + h][:, 0:DW * SGW],
                                                     parts[:, b, part, h * P:(h + 1) * P],
                                                     count_tile[:, t % ATILES, :, b % HTILE, :],
                                                     start=(b == 0 and part == 0), stop=(b == NB - 1 and part == 2))
                            if b == NB - 1 or b % HTILE == HTILE - 1:
                                last.then_inc(s_tile_used, 1)

                        def z_turn(j):
                            n = rows_of(j)
                            pe.wait_ge(s_h[j % HB], 16 * (j // HB + 1))
                            if j >= 1:
                                pe.wait_ge(s_hT_cp, j)
                            for h in range(DH):
                                last = pe.transpose(bank[6][:, h * P:(h + 1) * P],
                                                    h_in[:, j % HB, h * P:(h + 1) * P], ident[:])
                            last.then_inc(s_hT, 1)

                        def z_product(j):
                            pe.wait_ge(s_hT_cp, j + 1)
                            if j >= 1:
                                pe.wait_ge(s_take, j)
                            for h in range(DH):
                                last = pe.matmul(bank[7][:, 0:D], hT[:, j % 2, h * P:(h + 1) * P], wT[Wr][:, h, :],
                                                 start=(h == 0), stop=(h == DH - 1))
                            last.then_inc(s_z, 1)

                        def product(j):
                            b = order[j]
                            if last_group[b] >= 0:
                                pe.wait_ge(s_add, last_group[b] + 1)
                            if last_dense[b] >= 0:
                                pe.wait_ge(s_dense_added, last_dense[b] + 1)
                            if first:
                                if j >= 1:
                                    pe.wait_ge(s_rdeg, j)
                                    pe.wait_ge(s_take, j)
                                pe.matmul(bank[6][:, D:D + 2], seg_row[:, b * P:(b + 1) * P], pick[:, :],
                                          start=True, stop=True)
                            before = j if first else j - 1
                            if before >= 1:
                                pe.wait_ge(s_take, before)
                            for h in range(DH):
                                last = pe.matmul(sum_bank[j % 2][:, 0:D], agg[:, h, b * P:(b + 1) * P],
                                                 wT[Wl][:, h, :], start=(h == 0), stop=(h == DH - 1))
                            last.then_inc(s_a, 1)

                        def turn(b):
                            pe.wait_ge(s_take, b + 1)
                            if b >= 1:
                                pe.wait_ge(s_y, b)
                            for h in range(DH):
                                last = pe.transpose(bank[7][:, h * P:(h + 1) * P],
                                                    vec[:, b % 2, h * P:(h + 1) * P], ident[:])
                            last.then_inc(s_vT, 1)

                        def update(b):
                            pe.wait_ge(s_vT_cp, b + 1)
                            if b >= 1:
                                pe.wait_ge(s_y, b)
                            for h in range(DH):
                                last = pe.matmul(bank[7][:, 0:D], vT[:, b % 2, h * P:(h + 1) * P],
                                                 wT["upd"][:, h, :], start=(h == 0), stop=(h == DH - 1))
                            last.then_inc(s_o, 1)

                        for s in range(slots):
                            if first:
                                if s < NG:
                                    relations(s)
                                    for i in counts_at(s):
                                        count_product(i)
                                if 1 <= s <= NG:
                                    sums(s - 1)
                                for b in at(s, 0):
                                    product(b)
                                for b in at(s, 3):
                                    turn(b)
                                for b in at(s, 4):
                                    update(b)
                            else:
                                if 1 <= s <= groups:
                                    free(s - 1)
                                for j in at(s, -1):
                                    z_turn(j)
                                if s < groups:
                                    sums(s)
                                for u in range(units):
                                    if unit_slot[u] == s:
                                        dense_unit(u)
                                for j in at(s, 0):
                                    product(j)
                                    z_product(j)
                end_of_stage(s_rows, layer_sems)

        rounds = nc.values_load(rounds_int[0:1, 0:1], min_val=1, max_val=ROUNDS)
        with nc.If(rounds < 2):
            for k in range(4):
                one_round_layer(k)
        with nc.Else():
            for k in range(4):
                edge_pass(k)
                node_stage(k)
        pass0.close()


_INS = ["x", "src", "dst", "edge_type_500", "L0_gnn_relation_emb", "L0_gnn_msg_w", "L0_gnn_msg_b", "L0_gnn_upd_w",
        "L0_gnn_upd_b", "L0_gnn_gate_w", "L0_gnn_gate_b", "L1_gnn_W1l", "L1_gnn_b1l", "L1_gnn_W1r", "L1_gnn_W2l",
        "L1_gnn_b2l", "L1_gnn_W2r"]


def kernel(**inputs):
    import numpy as _np
    import concourse.bacc as _bacc
    from concourse import mybir as _mybir
    from concourse.bass_utils import run_bass_kernel_spmd as _run

    nc = _bacc.Bacc("TRN2", target_bir_lowering=False, num_devices=1)
    arrays, args = {}, []
    for name in _INS:
        a = _np.ascontiguousarray(inputs[name])
        arrays[f"in_{name}_dram"] = a
        args.append(nc.dram_tensor(f"in_{name}_dram", a.shape, _mybir.dt.from_np(a.dtype), kind="ExternalInput").ap())
    out = nc.dram_tensor("out_0_dram", inputs["x"].shape, _mybir.dt.float32, kind="ExternalOutput").ap()
    gnn_program(nc, *args, out)
    r = _run(nc, [arrays], core_ids=[0])
    return r.results[0]["out_0_dram"]
```
